# Optimizing a Trainium2 kernel written in Bass

```python
import numpy as np
import jax
import jax.numpy as jnp

def _softmax(x, axis=-1):
    return jax.nn.softmax(x, axis=axis)

def _gelu(x):
    return jax.nn.gelu(x, approximate=True)

def _silu(x):
    return jax.nn.silu(x)

def _sigmoid(x):
    return jax.nn.sigmoid(x)

def _layernorm(x, axis=-1, eps=1e-05):
    m = jnp.mean(x, axis=axis, keepdims=True)
    v = jnp.var(x, axis=axis, keepdims=True)
    return (x - m) / jnp.sqrt(v + eps)

def _scatter_add(tgt, idx, src, axis=0):
    return tgt.at[idx].add(src)

def _segment_sum(src, seg, n):
    return jax.ops.segment_sum(src, seg, n)
kernel_name = 'mk_gnn_preln_d2_gnn_r64_d02b62'

def setup_inputs(seed: int=0):
    np.random.seed(seed)
    _w = jnp.asarray

    def _rec_inputs():
        import jax
        import jax.numpy as jnp
        _gk = jax.random.key(seed)
        x = -0.000202 + 1 * jax.random.normal(jax.random.fold_in(_gk, 1), (50000, 128), jnp.float32)
        src = jax.random.randint(jax.random.fold_in(_gk, 2), (25000,), 0, 50000, jnp.int32)
        dst = jnp.minimum((50000 * jax.random.uniform(jax.random.fold_in(_gk, 3), (25000,)) ** 2.0).astype(jnp.int32), 49999)
        _o = jnp.argsort(dst, stable=True)
        src = src[_o]
        dst = dst[_o]
        edge_attr_128 = -5.16925e-05 + 1.00005 * jax.random.normal(jax.random.fold_in(_gk, 11), (25000, 128), jnp.float32)
        return (x, src, dst, edge_attr_128)
    x, src, dst, edge_attr_128 = _rec_inputs()

    def _L0_gnn_setup():
        import jax, jax.numpy as jnp
        import numpy as np
        N, E, F = (50000, 12500, 128)
        DELTA = 1.0
        EPS = 1e-05

        def _pna_forward(x, edge_index, W_pre, b_pre, W_post, b_post, W_lin, b_lin):
            src, dst = (edge_index[0], edge_index[1])
            n = x.shape[0]
            h = jnp.concatenate([x[dst], x[src]], axis=-1)
            m = h @ W_pre.T + b_pre
            deg = jax.ops.segment_sum(jnp.ones((m.shape[0],), m.dtype), dst, num_segments=n)
            deg_c = jnp.maximum(deg, 1.0)[:, None]
            has_edge = (deg > 0)[:, None]
            mx = jax.ops.segment_max(m, dst, num_segments=n)
            mx = jnp.where(has_edge, mx, 0.0)
            mn = jax.ops.segment_min(m, dst, num_segments=n)
            mn = jnp.where(has_edge, mn, 0.0)
            s1 = jax.ops.segment_sum(m, dst, num_segments=n)
            s2 = jax.ops.segment_sum(m * m, dst, num_segments=n)
            mean = s1 / deg_c
            var = s2 / deg_c - mean * mean
            std = jnp.sqrt(jax.nn.relu(var) + EPS)
            agg = jnp.concatenate([mx, mn, mean, std], axis=-1)
            log_deg = jnp.log(deg_c + 1.0)
            amp = log_deg / DELTA
            att = DELTA / log_deg
            scaled = jnp.concatenate([agg, agg * amp, agg * att], axis=-1)
            out = jnp.concatenate([x, scaled], axis=-1) @ W_post.T + b_post
            return out @ W_lin.T + b_lin
        key = jax.random.key(seed)
        ks = jax.random.split(key, 6)
        x = jax.random.normal(ks[0], (N, F), dtype=jnp.float32)
        edge_index = jax.random.randint(ks[1], (2, E), 0, N, dtype=jnp.int32)
        W_pre = jax.random.normal(ks[2], (F, 2 * F), dtype=jnp.float32) * (2 * F) ** (-0.5)
        b_pre = jnp.zeros((F,), jnp.float32)
        W_post = jax.random.normal(ks[3], (F, 13 * F), dtype=jnp.float32) * (13 * F) ** (-0.5)
        b_post = jnp.zeros((F,), jnp.float32)
        W_lin = jax.random.normal(ks[4], (F, F), dtype=jnp.float32) * F ** (-0.5)
        b_lin = jnp.zeros((F,), jnp.float32)
        return {'x': x, 'edge_index': edge_index, 'W_pre': W_pre, 'b_pre': b_pre, 'W_post': W_post, 'b_post': b_post, 'W_lin': W_lin, 'b_lin': b_lin}
    _L0_gnn_all = _L0_gnn_setup()
    _L0_gnn_in = {k: v for k, v in _L0_gnn_all.items() if k in ('W_pre', 'b_pre', 'W_post', 'b_post', 'W_lin', 'b_lin')}
    del _L0_gnn_all

    def _L1_gnn_setup():
        import jax, jax.numpy as jnp
        import numpy as np
        N_NODES = 50000
        N_EDGES = 12500
        F_X = 128
        F_E = 128
        HID = 256
        F_OUT = 128
        key = jax.random.key(seed)
        k1, k2, k3, k4, k5 = jax.random.split(key, 5)
        x = jax.random.normal(k1, (N_NODES, F_X), dtype=jnp.float32)
        edge_index = jax.random.randint(k2, (2, N_EDGES), 0, N_NODES, dtype=jnp.int64)
        edge_attr = jax.random.normal(k3, (N_EDGES, F_E), dtype=jnp.float32)
        din = F_X + F_E
        W1 = jax.random.normal(k4, (din, HID), dtype=jnp.float32) * (1.0 / np.sqrt(din))
        b1 = jnp.zeros((HID,), dtype=jnp.float32)
        W2 = jax.random.normal(k5, (HID, F_OUT), dtype=jnp.float32) * (1.0 / np.sqrt(HID))
        b2 = jnp.zeros((F_OUT,), dtype=jnp.float32)
        return {'x': x, 'edge_index': edge_index, 'edge_attr': edge_attr, 'W1': W1, 'b1': b1, 'W2': W2, 'b2': b2}
    _L1_gnn_all = _L1_gnn_setup()
    _L1_gnn_in = {k: v for k, v in _L1_gnn_all.items() if k in ('W1', 'b1', 'W2', 'b2')}
    del _L1_gnn_all
    return {'x': x, 'src': src, 'dst': dst, 'edge_attr_128': edge_attr_128, 'L0_gnn_W_pre': _L0_gnn_in['W_pre'], 'L0_gnn_b_pre': _L0_gnn_in['b_pre'], 'L0_gnn_W_post': _L0_gnn_in['W_post'], 'L0_gnn_b_post': _L0_gnn_in['b_post'], 'L0_gnn_W_lin': _L0_gnn_in['W_lin'], 'L0_gnn_b_lin': _L0_gnn_in['b_lin'], 'L1_gnn_W1': _L1_gnn_in['W1'], 'L1_gnn_b1': _L1_gnn_in['b1'], 'L1_gnn_W2': _L1_gnn_in['W2'], 'L1_gnn_b2': _L1_gnn_in['b2']}

def reference(x, src, dst, edge_attr_128, L0_gnn_W_pre, L0_gnn_b_pre, L0_gnn_W_post, L0_gnn_b_post, L0_gnn_W_lin, L0_gnn_b_lin, L1_gnn_W1, L1_gnn_b1, L1_gnn_W2, L1_gnn_b2):
    import jax
    import jax.numpy as jnp

    def _L0_gnn_ref(x, edge_index, W_pre, b_pre, W_post, b_post, W_lin, b_lin):
        import jax, jax.numpy as jnp
        import numpy as np
        N, E, F = (50000, 12500, 128)
        DELTA = 1.0
        EPS = 1e-05

        def _pna_forward(x, edge_index, W_pre, b_pre, W_post, b_post, W_lin, b_lin):
            src, dst = (edge_index[0], edge_index[1])
            n = x.shape[0]
            h = jnp.concatenate([x[dst], x[src]], axis=-1)
            m = h @ W_pre.T + b_pre
            deg = jax.ops.segment_sum(jnp.ones((m.shape[0],), m.dtype), dst, num_segments=n)
            deg_c = jnp.maximum(deg, 1.0)[:, None]
            has_edge = (deg > 0)[:, None]
            mx = jax.ops.segment_max(m, dst, num_segments=n)
            mx = jnp.where(has_edge, mx, 0.0)
            mn = jax.ops.segment_min(m, dst, num_segments=n)
            mn = jnp.where(has_edge, mn, 0.0)
            s1 = jax.ops.segment_sum(m, dst, num_segments=n)
            s2 = jax.ops.segment_sum(m * m, dst, num_segments=n)
            mean = s1 / deg_c
            var = s2 / deg_c - mean * mean
            std = jnp.sqrt(jax.nn.relu(var) + EPS)
            agg = jnp.concatenate([mx, mn, mean, std], axis=-1)
            log_deg = jnp.log(deg_c + 1.0)
            amp = log_deg / DELTA
            att = DELTA / log_deg
            scaled = jnp.concatenate([agg, agg * amp, agg * att], axis=-1)
            out = jnp.concatenate([x, scaled], axis=-1) @ W_post.T + b_post
            return out @ W_lin.T + b_lin
        return _pna_forward(x, edge_index, W_pre, b_pre, W_post, b_post, W_lin, b_lin)

    def _L1_gnn_ref(x, edge_index, edge_attr, W1, b1, W2, b2):
        import jax, jax.numpy as jnp
        import numpy as np
        N_NODES = 50000
        N_EDGES = 12500
        F_X = 128
        F_E = 128
        HID = 256
        F_OUT = 128
        num_nodes = x.shape[0]
        dst = edge_index[1]
        sums = jax.ops.segment_sum(edge_attr, dst, num_segments=num_nodes)
        ones = jnp.ones((edge_attr.shape[0],), dtype=edge_attr.dtype)
        counts = jax.ops.segment_sum(ones, dst, num_segments=num_nodes)
        agg = sums / jnp.maximum(counts, 1.0)[:, None]
        node_inputs = jnp.concatenate([x, agg], axis=-1)
        h = jax.nn.relu(node_inputs @ W1 + b1)
        return h @ W2 + b2
    edge_index = jnp.stack([src, dst])
    h = jnp.maximum(_layernorm(x, axis=-1), 0.0)
    x = x + _L0_gnn_ref(h, edge_index, L0_gnn_W_pre, L0_gnn_b_pre, L0_gnn_W_post, L0_gnn_b_post, L0_gnn_W_lin, L0_gnn_b_lin)
    h = jnp.maximum(_layernorm(x, axis=-1), 0.0)
    x = x + _L1_gnn_ref(h, edge_index, edge_attr_128, L1_gnn_W1, L1_gnn_b1, L1_gnn_W2, L1_gnn_b2)
    return x

_drawn_inputs = setup_inputs


def setup_inputs(seed=0):
    import zlib

    import numpy as np

    out = dict(_drawn_inputs(seed))
    spreads = {'L0_gnn_b_pre': (0.0, 0.1),
     'L0_gnn_b_post': (0.0, 0.1),
     'L0_gnn_b_lin': (0.0, 0.1),
     'L1_gnn_b1': (0.0, 0.1),
     'L1_gnn_b2': (0.0, 0.1)}
    factors = {}
    for name, (base, spread) in spreads.items():
        noise = np.random.default_rng([zlib.crc32(name.encode()), seed]).standard_normal(out[name].shape)
        drawn = base * np.exp(spread * noise) if base else spread * noise
        out[name] = jnp.asarray(drawn.astype(out[name].dtype))
    for name, factor in factors.items():
        out[name] = (out[name] * factor).astype(out[name].dtype)
    return out
```

```python
import math

import concourse.bass as bass
from concourse import mybir

ALU = mybir.AluOpType
ACT = mybir.ActivationFunctionType
F32 = mybir.dt.float32
BF16 = mybir.dt.bfloat16
I32 = mybir.dt.int32

P = 128
TILES = 4
CHUNK = P * TILES
LN_EPS = 1e-5
STD_EPS = 1e-5
FAR = 1 << 20
RESET = -3.0e38
AGGS = 4
SCALERS = 3
MX, MN, ME, SD = range(AGGS)


def build(nc, x, src, dst, edge_attr, w_pre, b_pre, w_post, b_post, w_lin, b_lin, w1, b1, w2, b2, out):
    N, F = x.shape
    E = src.shape[0]
    HID = w1.shape[1]
    assert F == P and HID == 2 * P and N >= CHUNK and N < FAR
    NODE_CHUNKS = -(-N // CHUNK)
    EDGE_CHUNKS = -(-E // CHUNK)
    ROWS = 2 * EDGE_CHUNKS
    RW = 2 * P
    FULL_ROWS = E // RW
    REST = E - FULL_ROWS * RW
    assert ROWS <= P and FULL_ROWS == ROWS - 1 and REST > 0
    LAST_EDGE_ROWS = E - (EDGE_CHUNKS - 1) * CHUNK

    keep_row = nc.dram_tensor("keep_row", [ROWS * RW], BF16, kind="Internal").ap()
    reset_row = nc.dram_tensor("reset_row", [ROWS * RW], BF16, kind="Internal").ap()
    lift_row = nc.dram_tensor("lift_row", [ROWS * RW], BF16, kind="Internal").ap()
    inv_row = nc.dram_tensor("inv_row", [ROWS * RW], F32, kind="Internal").ap()

    def sb(name, shape, dt=F32):
        return nc.alloc_sbuf_tensor(name, shape, dt)

    bank = [nc.alloc_psum_tensor(f"bank{i}", [P, CHUNK], F32) for i in range(8)]
    sems = {}

    def sem(name):
        if name not in sems:
            sems[name] = nc.alloc_semaphore(name)
        return sems[name]

    ident = sb("ident", [P, P])
    w_pre_sb = sb("w_pre_sb", [P, 2 * P])
    attr = sb("attr", [P, 4, TILES, P])
    w_post_sb = attr[:].rearrange("p s j f -> p (s j f)")[:, 0:13 * P]
    w_lin_sb = sb("w_lin_sb", [P, P])
    w_lin_t = sb("w_lin_t", [P, P])
    wd_t = sb("wd_t", [P, P])
    ws_t = sb("ws_t", [P, P])
    comb_x = sb("comb_x", [P, P])
    comb_agg = sb("comb_agg", [P, AGGS, SCALERS, P])
    w1_sb = sb("w1_sb", [P, 2, HID])
    w2_sb = sb("w2_sb", [P, 2, P])
    b1_col = sb("b1_col", [P, 2])
    b_pre_col = sb("b_pre_col", [P, 1])
    b_post_col = sb("b_post_col", [P, 1])
    b_post_wide = sb("b_post_wide", [P, P])
    b_lin_all = sb("b_lin_all", [P, P])
    b2_all = sb("b2_all", [P, TILES, P])
    edge_const = sb("edge_const", [P, TILES, P])
    lone_const = sb("lone_const", [P, TILES, P])
    lone_std = sb("lone_std", [P, SCALERS, P])
    eps_col = sb("eps_col", [P, 1])

    dst_i = sb("dst_i", [P, RW + 2], I32)
    src_i = sb("src_i", [P, RW], I32)
    pos_i = sb("pos_i", [P, RW], I32)
    dst_f = sb("dst_f", [P, RW + 2])
    agg = sb("agg", [P, 2, AGGS, CHUNK])
    work = agg[:].rearrange("p b a (n w) -> p (b a n) w", w=RW)
    first = work[:, 0, :]
    final = work[:, 1, :]
    pos1 = work[:, 2, :]
    start_mark = work[:, 3, :]
    start_scan = work[:, 4, :]
    seg_start = work[:, 5, :]
    row_max = sb("row_max", [1, P])
    row_carry = sb("row_carry", [1, P])
    carry_col = sb("carry_col", [P, 1])
    count = work[:, 6, :]
    inv_count = sb("inv_count", [P, RW])
    keep_sb = sb("keep_sb", [P, RW], BF16)
    reset_sb = sb("reset_sb", [P, RW], BF16)
    lift_sb = sb("lift_sb", [P, RW], BF16)
    far_sb = work[:, 7, :]
    far_diff = work[:, 8, :]
    far_pick = work[:, 9, :]
    to_turn = work[:, 10:15, :]
    index = sb("index", [P, 3, ROWS, 2], I32)
    scale = sb("scale", [P, 2, ROWS, 2])

    nx = sb("nx", [P, 2, TILES, P])
    nxc = sb("nxc", [P, 2, TILES, P])
    nh = sb("nh", [P, 2, TILES, P])
    nht = sb("nht", [P, 2, CHUNK])
    nx1 = sb("nx1", [P, 2, TILES, P])
    nx1b = sb("nx1b", [P, 2, TILES, P])
    nh2 = sb("nh2", [P, 2, TILES, P])
    nh2t = sb("nh2t", [P, 2, CHUNK])
    nut = sb("nut", [P, 2, 2, CHUNK])
    nout = sb("nout", [P, 2, TILES, P])
    nbn1 = sb("nbn1", [P, 2, TILES, 6])
    nmv1 = sb("nmv1", [P, 2, TILES, 2])
    nsd1 = sb("nsd1", [P, 2, TILES])
    nrs1 = sb("nrs1", [P, 2, TILES])
    nbn2 = sb("nbn2", [P, 2, TILES, 6])
    nmv2 = sb("nmv2", [P, 2, TILES, 2])
    nsd2 = sb("nsd2", [P, 2, TILES])
    nrs2 = sb("nrs2", [P, 2, TILES])

    xs = sb("xs", [P, 4, TILES, P])
    xd = sb("xd", [P, 4, TILES, P])
    xdc = sb("xdc", [P, 4, TILES, P])
    keep = sb("keep", [P, 4, CHUNK], BF16)
    reset = sb("reset", [P, 4, CHUNK], BF16)
    lift = sb("lift", [P, 4, CHUNK], BF16)
    inv = sb("inv", [P, 4, CHUNK])
    idx = sb("idx", [P, 4, 3, TILES], I32)
    oidx = sb("oidx", [P, 4, TILES], I32)
    amp_att = sb("amp_att", [P, 4, 2, TILES])
    bn1 = sb("bn1", [P, 2, 2 * TILES, 6])
    mv1 = sb("mv1", [P, 2, 2 * TILES, 2])
    sd1 = sb("sd1", [P, 2, 2 * TILES])
    rs1 = sb("rs1", [P, 2, 2 * TILES])
    hs = sb("hs", [P, 2, TILES, P])
    hd = sb("hd", [P, 2, TILES, P])
    hst = sb("hst", [P, 2, CHUNK])
    hdt = sb("hdt", [P, 2, CHUNK])
    bsq = sb("bsq", [P, 2, CHUNK])
    run_max = sb("run_max", [P, 2, CHUNK])
    run_min = sb("run_min", [P, 2, CHUNK])
    run_sum = sb("run_sum", [P, 2, CHUNK])
    run_sq = sb("run_sq", [P, 2, CHUNK])
    run_attr = sb("run_attr", [P, 2, CHUNK])
    mean_b = sb("mean_b", [P, CHUNK])
    mean_b2 = sb("mean_b2", [P, CHUNK])
    sq_mean = sb("sq_mean", [P, CHUNK])
    var = sb("var", [P, CHUNK])
    var_pos = sb("var_pos", [P, CHUNK])
    attr_mean = sb("attr_mean", [P, 2, CHUNK])
    part = sb("part", [P, 2, P])
    part2 = sb("part2", [P, 2, P])
    x1 = nx1
    x1b = nx1b
    bn2 = sb("bn2", [P, 2, TILES, 6])
    mv2 = sb("mv2", [P, 2, TILES, 2])
    sd2 = sb("sd2", [P, 2, TILES])
    rs2 = sb("rs2", [P, 2, TILES])
    h2 = nh2
    h2t = nh2t
    ut = nut
    eout = nout

    def pipeline(eng, step, lo, hi, loop_lo, loops, unroll):
        for k in range(lo, loop_lo):
            step(k, 0)
        with eng.Fori(0, loops) as i:
            for u in range(unroll):
                step(loop_lo + u, i)
        for k in range(loop_lo + loops * unroll, hi):
            step(k, 0)

    NU, EU = 2, 4
    N_LO, N_HI = -4, NODE_CHUNKS + 1
    N_LOOP = 4
    N_LOOPS = (NODE_CHUNKS - 5 - N_LOOP) // NU
    E_LO, E_HI = -4, EDGE_CHUNKS + 2
    E_LOOP = 4
    E_LOOPS = (EDGE_CHUNKS - 5 - E_LOOP) // EU

    def node_pipeline(eng, step):
        pipeline(eng, step, N_LO, N_HI, N_LOOP, N_LOOPS, NU)

    def edge_pipeline(eng, step):
        pipeline(eng, step, E_LO, E_HI, E_LOOP, E_LOOPS, EU)

    def node(c):
        return 0 <= c < NODE_CHUNKS

    def edge(c):
        return 0 <= c < EDGE_CHUNKS

    def node_rows(ap, c, i):
        base = min(c * CHUNK, N - CHUNK) + i * (NU * CHUNK)
        return ap[bass.ds(base, CHUNK), :].rearrange("(p j) f -> p j f", j=TILES)

    with nc.Block() as block:

        @block.sync
        def _(sp):
            w = sem("weights_in")
            sp.dma_start(w_lin_sb[:], w_lin).then_inc(w, 16)
            sp.dma_start(w_pre_sb[:], w_pre).then_inc(w, 16)
            sp.dma_start(w_post_sb, w_post).then_inc(w, 16)
            sp.dma_start(w1_sb[:], w1.rearrange("(k p) h -> p k h", p=P)).then_inc(w, 16)
            sp.dma_start(w2_sb[:], w2.rearrange("(k p) h -> p k h", p=P)).then_inc(w, 16)
            sp.dma_start(b_lin_all[:], b_lin.rearrange("(a f) -> a f", a=1).to_broadcast([P, P])).then_inc(w, 16)
            for j in range(TILES):
                sp.dma_start(b2_all[:, j, :], b2.rearrange("(a f) -> a f", a=1).to_broadcast([P, P])).then_inc(w, 16)
            with nc.allow_non_contiguous_dma(reason="a bias as one value per partition"):
                sp.dma_start(b1_col[:], b1.rearrange("(k p) -> p k", p=P)).then_inc(w, 16)
                sp.dma_start(b_pre_col[:], b_pre.rearrange("(p a) -> p a", a=1)).then_inc(w, 16)
                sp.dma_start(b_post_col[:], b_post.rearrange("(p a) -> p a", a=1)).then_inc(w, 16)

            sp.wait_ge(sem("pad_written"), 1)
            e = sem("edge_list_in")
            d = dst.tensor
            sp.dma_start(dst_i[0:1, 1:RW + 2], bass.AP(tensor=d, offset=0, ap=[[RW + 1, 1], [1, RW + 1]])).then_inc(e, 16)
            sp.dma_start(dst_i[1:FULL_ROWS, :],
                         bass.AP(tensor=d, offset=RW - 1, ap=[[RW, FULL_ROWS - 1], [1, RW + 2]])).then_inc(e, 16)
            sp.dma_start(dst_i[FULL_ROWS:ROWS, 0:REST + 1],
                         bass.AP(tensor=d, offset=FULL_ROWS * RW - 1, ap=[[REST + 1, 1], [1, REST + 1]])).then_inc(e, 16)
            sp.dma_start(src_i[0:FULL_ROWS, :], src[0:FULL_ROWS * RW].rearrange("(r w) -> r w", w=RW)).then_inc(e, 16)
            sp.dma_start(src_i[FULL_ROWS:ROWS, 0:REST],
                         src[FULL_ROWS * RW:E].rearrange("(a w) -> a w", a=1)).then_inc(e, 16)

            sp.wait_ge(sem("masks_done"), 1)
            r = sem("rows_out")
            sp.dma_start(keep_row.rearrange("(r w) -> r w", w=RW), keep_sb[0:ROWS, :]).then_inc(r, 16)
            sp.dma_start(reset_row.rearrange("(r w) -> r w", w=RW), reset_sb[0:ROWS, :]).then_inc(r, 16)
            sp.dma_start(lift_row.rearrange("(r w) -> r w", w=RW), lift_sb[0:ROWS, :]).then_inc(r, 16)
            sp.dma_start(inv_row.rearrange("(r w) -> r w", w=RW), inv_count[0:ROWS, :]).then_inc(r, 16)

            def node_step(k, i):
                c = k + 4
                if node(c):
                    if c >= 2:
                        sp.wait_ge(sem("n_norm1"), c - 1 + NU * i)
                        sp.wait_ge(sem("n_xc"), c - 1 + NU * i)
                    sp.dma_start(nx[:, c % 2], node_rows(x, c, i)).then_inc(sem(f"n_in{c % 2}"), 16)
                c = k - 1
                if node(c):
                    sp.wait_ge(sem("n_out"), c + 1 + NU * i)
                    if c == NODE_CHUNKS - 1:
                        sp.wait_ge(sem(f"n_stored{(c - 1) % 2}"), 16 * ((c - 1) // 2 + 1))
                    sp.dma_start(node_rows(out, c, i), nout[:, c % 2]).then_inc(sem(f"n_stored{c % 2}"), 16)

            node_pipeline(sp, node_step)

            sp.wait_ge(r, 64)

            def edge_step(k, i):
                c = k + 4
                if edge(c):
                    s = c % 4
                    if c >= 4:
                        sp.wait_ge(sem("e_attr_mean"), c - 3 + EU * i)
                        sp.wait_ge(sem("e_turned_attr"), c - 3 + EU * i)
                    m = sem(f"e_masks_in{s}")
                    for dst_sb, row in ((keep, keep_row), (reset, reset_row), (lift, lift_row), (inv, inv_row)):
                        sp.dma_start(dst_sb[:, s, :],
                                     row[bass.ds(c * CHUNK + i * (EU * CHUNK), CHUNK)]
                                     .rearrange("(a w) -> a w", a=1).to_broadcast([P, CHUNK])).then_inc(m, 16)
                    a = sem(f"e_attr_in{s}")
                    if c < EDGE_CHUNKS - 1:
                        rows = edge_attr[bass.ds(c * CHUNK + i * (EU * CHUNK), CHUNK), :]
                        sp.dma_start(attr[:, s], rows.rearrange("(j p) f -> p j f", p=P)).then_inc(a, 16)
                    else:
                        whole = LAST_EDGE_ROWS // P
                        base = c * CHUNK
                        sp.dma_start(attr[:, s, 0:whole, :],
                                     edge_attr[base:base + whole * P, :].rearrange("(j p) f -> p j f", p=P)).then_inc(a, 16)
                        sp.dma_start(attr[0:LAST_EDGE_ROWS - whole * P, s, whole, :],
                                     edge_attr[base + whole * P:E, :]).then_inc(a, 16)

            edge_pipeline(sp, edge_step)

        @block.gpsimd
        def _(pool):
            fixed = sem("ident_ready")
            pool.memset(ident[:], 0.0).then_inc(sem("ident_zero"), 1)
            pool.iota(pos_i[:], pattern=[[1, RW]], base=1, channel_multiplier=RW).then_inc(sem("pos_ready"), 1)
            pool.wait_ge(sem("ident_zero"), 1)
            pool.affine_select(out=ident[:], in_=ident[:], compare_op=ALU.not_equal, fill=1.0, base=0,
                               pattern=[[-1, P]], channel_multiplier=1).then_inc(sem("ident_ready"), 1)
            pool.wait_ge(sem("const_ready"), 2 * TILES)

            def node_step(k, i):
                c = k + 2
                if node(c):
                    pool.wait_ge(sem(f"n_in{c % 2}"), 16 * (c // 2 + 1) + 16 * i)
                    if c >= 2:
                        pool.wait_ge(sem("n_x1"), c - 1 + NU * i)
                    pool.tensor_tensor(nxc[:, c % 2], nx[:, c % 2], lone_const[:], ALU.add).then_inc(sem("n_xc"), 1)
                c = k + 1
                if node(c):
                    pool.wait_ge(sem("n_x1"), c + 1 + NU * i)
                    if c >= 2:
                        pool.wait_ge(sem("n_out"), c - 1 + NU * i)
                    if c == 0:
                        pool.wait_ge(sem("weights_in"), 16 * 13)
                    pool.tensor_tensor(nx1b[:, c % 2], nx1[:, c % 2], b2_all[:], ALU.add).then_inc(sem("n_x1b"), 1)

            node_pipeline(pool, node_step)

            pool.wait_ge(sem("turned_out"), 10)

            def edge_step(k, i):
                c = k - 1
                if edge(c):
                    pool.wait_ge(sem("e_mixed"), TILES * (c + 1) + TILES * EU * i)
                    if c >= 2:
                        pool.wait_ge(sem("e_out"), c - 1 + EU * i)
                    pool.tensor_tensor(x1b[:, c % 2], x1[:, c % 2], b2_all[:], ALU.add).then_inc(sem("e_x1b"), 1)
                c = k + 2
                if edge(c):
                    pool.wait_ge(sem(f"e_gathered{c % 4}"), 16 * 2 * TILES * (c // 4 + 1) + 16 * 2 * TILES * i)
                    if c >= 4:
                        pool.wait_ge(sem("e_mixed"), TILES * (c - 3) + TILES * EU * i)
                    pool.tensor_tensor(xdc[:, c % 4], xd[:, c % 4], edge_const[:], ALU.add).then_inc(sem("e_xdc"), 1)
                c = k - 2
                if edge(c):
                    pool.wait_ge(fixed, 1)
                    pool.wait_ge(sem("e_out"), c + 1 + EU * i)
                    if c == 0:
                        for n in range(2):
                            pool.wait_ge(sem(f"n_stored{n}"), 16 * ((NODE_CHUNKS - n + 1) // 2))
                    if c >= 4:
                        pool.wait_ge(sem(f"e_scattered{c % 4}"), 16 * TILES * (c // 4) + 16 * TILES * i)
                    t = bass.ds(2 * c + (2 * EU) * i, 2)
                    pool.tensor_copy(oidx[:, c % 4].rearrange("p (r h) -> p r h", h=2), index[:, 2, t, :]).then_inc(sem("e_oidx"), 1)
                c = k + 4
                if edge(c):
                    s = c % 4
                    pool.wait_ge(fixed, 1)
                    if c >= 4:
                        pool.wait_ge(sem(f"e_gathered{s}"), 16 * 2 * TILES * (c // 4) + 16 * 2 * TILES * i)
                        pool.wait_ge(sem("e_mixed"), TILES * (c - 3) + TILES * EU * i)
                        pool.wait_ge(sem("e_norm1"), c - 3 + EU * i)
                        pool.wait_ge(sem("e_xdc"), c - 3 + EU * i)
                    t = bass.ds(2 * c + (2 * EU) * i, 2)
                    pool.tensor_copy(idx[:, s].rearrange("p w (r h) -> p w r h", h=2), index[:, :, t, :]).then_inc(sem("e_idx"), 1)
                    pool.wait_ge(sem("e_idx"), c + 1 + EU * i)
                    if edge(k - 2):
                        pool.wait_ge(sem("e_oidx"), k - 1 + EU * i)
                    pool.tensor_copy(amp_att[:, s].rearrange("p w (r h) -> p w r h", h=2), scale[:, :, t, :]).then_inc(sem("e_scale"), 1)
                    g = sem(f"e_gathered{s}")
                    for j in range(TILES):
                        for which, rows in ((0, xs), (1, xd)):
                            pool.indirect_dma_start(
                                out=rows[:, s, j, :], out_offset=None, in_=x,
                                in_offset=bass.IndirectOffsetOnAxis(ap=idx[:, s, which, j:j + 1], axis=0)).then_inc(g, 16)
                c = k - 2
                if edge(c):
                    if not edge(k + 4):
                        pool.wait_ge(sem("e_oidx"), k - 1)
                    for j in range(TILES):
                        pool.indirect_dma_start(
                            out=out, out_offset=bass.IndirectOffsetOnAxis(ap=oidx[:, c % 4, j:j + 1], axis=0),
                            in_=eout[:, c % 2, j, :], in_offset=None,
                            bounds_check=N - 1, oob_is_err=False).then_inc(sem(f"e_scattered{c % 4}"), 16)

            edge_pipeline(pool, edge_step)
            for s in range(4):
                pool.wait_ge(sem(f"e_scattered{s}"), 16 * TILES * ((EDGE_CHUNKS - s + 3) // 4))

        @block.tensor
        def _(pe):
            pe.wait_ge(sem("ident_ready"), 1)
            pe.wait_ge(sem("weights_in"), 16 * 13)
            pe.transpose(bank[0][:, 0:P], w_lin_sb[:], ident[:])
            pe.transpose(bank[0][:, P:2 * P], w_pre_sb[:, 0:P], ident[:])
            pe.transpose(bank[0][:, 2 * P:3 * P], w_pre_sb[:, P:2 * P], ident[:]).then_inc(sem("weights_turned"), 1)
            pe.wait_ge(sem("weights_copied"), 1)
            for b in range(13):
                mm = pe.matmul(bank[1 + b // 4][:, b % 4 * P:(b % 4 + 1) * P], w_post_sb[:, b * P:(b + 1) * P], w_lin_t[:],
                               start=True, stop=True)
            mm.then_inc(sem("comb_ready"), 1)
            pe.wait_ge(sem("b_post_ready"), 1)
            pe.matmul(bank[5][:, 0:P], b_post_wide[:], w_lin_t[:], start=True, stop=True).then_inc(sem("const_psum"), 1)
            pe.wait_ge(sem("comb_copied"), 1)
            pe.wait_ge(sem("lone_std_ready"), 1)
            for s in range(SCALERS):
                mm = pe.matmul(bank[6][:, 0:P], lone_std[:, s, :], comb_agg[:, SD, s, :], start=(s == 0), stop=(s == SCALERS - 1))
            mm.then_inc(sem("const_psum"), 1)
            pe.wait_ge(sem("start_scanned"), 1)
            pe.transpose(bank[7][0:1, 0:ROWS], start_scan[0:ROWS, RW - 1:RW], ident[0:ROWS, 0:ROWS]).then_inc(sem("row_max_psum"), 1)
            pe.wait_ge(sem("row_carry_ready"), 1)
            pe.transpose(bank[7][0:ROWS, P:P + 1], row_carry[0:1, 0:ROWS], ident[0:1, 0:1]).then_inc(sem("carry_psum"), 1)
            for n in range(5):
                pe.wait_ge(sem("to_turn_ready"), n + 1)
                for h in range(2):
                    if 2 * n + h >= 2:
                        pe.wait_ge(sem("turned_out"), 2 * n + h - 1)
                    pe.transpose(bank[h][:, 0:ROWS], to_turn[0:ROWS, n, h * P:(h + 1) * P],
                                 ident[0:ROWS, 0:ROWS]).then_inc(sem("turned"), 1)
            pe.wait_ge(sem("turned_out"), 10)

            def node_step(k, i):
                c = k + 1
                if node(c):
                    pe.wait_ge(sem("n_norm1"), c + 1 + NU * i)
                    if c >= 1:
                        pe.wait_ge(sem("n_ht"), c + NU * i)
                    for j in range(TILES):
                        mm = pe.transpose(bank[0][:, j * P:(j + 1) * P], nh[:, c % 2, j, :], ident[:])
                    mm.then_inc(sem("n_turn1"), 1)
                c = k - 1
                if node(c):
                    pe.wait_ge(sem("n_ut"), 2 * (c + 1) + 2 * NU * i)
                    if c >= 1:
                        pe.wait_ge(sem("n_out"), c + NU * i)
                    for j in range(TILES):
                        for m in range(2):
                            mm = pe.matmul(bank[5][:, j * P:(j + 1) * P], nut[:, c % 2, m, j * P:(j + 1) * P], w2_sb[:, m, :],
                                           start=(m == 0), stop=(m == 1))
                    mm.then_inc(sem("n_out_psum"), 1)
                c = k
                if node(c):
                    pe.wait_ge(sem("n_norm2"), c + 1 + NU * i)
                    if c >= 1:
                        pe.wait_ge(sem("n_h2t"), c + NU * i)
                    for j in range(TILES):
                        mm = pe.transpose(bank[2][:, j * P:(j + 1) * P], nh2[:, c % 2, j, :], ident[:])
                    mm.then_inc(sem("n_turn2"), 1)
                c = k + 1
                if node(c):
                    pe.wait_ge(sem("n_ht"), c + 1 + NU * i)
                    if c >= 1:
                        pe.wait_ge(sem("n_x1"), c + NU * i)
                    for j in range(TILES):
                        mm = pe.matmul(bank[1][:, j * P:(j + 1) * P], nht[:, c % 2, j * P:(j + 1) * P], comb_x[:],
                                       start=True, stop=True)
                    mm.then_inc(sem("n_y_psum"), 1)
                c = k
                if node(c):
                    pe.wait_ge(sem("n_h2t"), c + 1 + NU * i)
                    for m in range(2):
                        if c >= 1:
                            pe.wait_ge(sem("n_ut"), 2 * c - 1 + m + 2 * NU * i)
                        pe.matmul(bank[3 + m][:], w1_sb[:, 0, m * P:(m + 1) * P], nh2t[:, c % 2, :],
                                  start=True, stop=True).then_inc(sem("n_u_psum"), 1)

            node_pipeline(pe, node_step)
            pe.wait_ge(sem("n_out"), NODE_CHUNKS)
            pe.wait_ge(sem("n_ut"), 2 * NODE_CHUNKS)

            def layer0(c, j, i):
                acc = bank[5 + j % 2]
                if j >= 2:
                    pe.wait_ge(sem("e_mixed"), TILES * c + j - 1 + TILES * EU * i)
                elif c >= 1:
                    pe.wait_ge(sem("e_mixed"), TILES * (c - 1) + j + 3 + TILES * EU * i)
                cols = slice(j * P, (j + 1) * P)
                for a in range(AGGS):
                    if j == 0:
                        pe.wait_ge(sem(f"e_agg{a}"), c + 1 + EU * i)
                    pe.matmul(acc[:, 0:SCALERS * P], agg[:, c % 2, a, cols],
                              comb_agg[:, a].rearrange("p s f -> p (s f)"), start=(a == 0), stop=False,
                              skip_group_check=True)
                pe.matmul(acc[:, 0:P], hdt[:, c % 2, cols], comb_x[:], start=False, stop=True,
                          skip_group_check=True).then_inc(sem("e_layer0"), 1)

            def edge_step(k, i):
                c = k + 1
                if edge(c):
                    pe.wait_ge(sem("e_norm1"), c + 1 + EU * i)
                    if c >= 2:
                        pe.wait_ge(sem("e_out"), c - 2 + 1 - 1 + EU * i) if c >= 3 else None
                    for j in range(TILES):
                        mm = pe.transpose(bank[0][:, j * P:(j + 1) * P], hs[:, c % 2, j, :], ident[:])
                    mm.then_inc(sem("e_turned_s"), 1)
                    if c >= 3:
                        pe.wait_ge(sem("e_ut"), 2 * (c - 2) + 2 * EU * i)
                    for j in range(TILES):
                        mm = pe.transpose(bank[1][:, j * P:(j + 1) * P], hd[:, c % 2, j, :], ident[:])
                    mm.then_inc(sem("e_turned_d"), 1)
                c = k
                if edge(c):
                    pe.wait_ge(sem(f"e_attr_in{c % 4}"),
                               16 * (c // 4 + 1) + 16 * i + (16 if c == EDGE_CHUNKS - 1 else 0))
                    if c >= 1:
                        pe.wait_ge(sem("e_attr_run"), c + EU * i)
                    for j in range(TILES):
                        mm = pe.transpose(bank[2][:, j * P:(j + 1) * P], attr[:, c % 4, j, :], ident[:])
                    mm.then_inc(sem("e_turned_attr"), 1)
                    layer0(c, 0, i)
                c = k + 1
                if edge(c):
                    pe.wait_ge(sem("e_hst"), c + 1 + EU * i)
                    if c >= 1:
                        pe.wait_ge(sem("e_sum"), c + EU * i)
                        pe.wait_ge(sem("e_bsq"), c + EU * i)
                    pe.matmul(bank[3][:], ws_t[:], hst[:, c % 2, :], start=True, stop=True).then_inc(sem("e_b_psum"), 1)
                    pe.wait_ge(sem("e_hdt"), c + 1 + EU * i)
                    if c >= 1:
                        pe.wait_ge(sem(f"e_agg{ME}"), c + EU * i)
                    pe.matmul(bank[4][:], wd_t[:], hdt[:, c % 2, :], start=True, stop=True).then_inc(sem("e_a_psum"), 1)
                c = k - 1
                if edge(c):
                    pe.wait_ge(sem("e_norm2"), c + 1 + EU * i)
                    if not edge(k + 1) and c >= 1:
                        pe.wait_ge(sem("e_out"), c + EU * i)
                    for j in range(TILES):
                        mm = pe.transpose(bank[0][:, j * P:(j + 1) * P], h2[:, c % 2, j, :], ident[:])
                    mm.then_inc(sem("e_turned2"), 1)
                c = k
                if edge(c):
                    layer0(c, 1, i)
                c = k - 1
                if edge(c):
                    pe.wait_ge(sem("e_h2t"), c + 1 + EU * i)
                    pe.wait_ge(sem("e_attr_mean"), c + 1 + EU * i)
                    for m, b in ((0, 7), (1, 1)):
                        if c >= 1:
                            pe.wait_ge(sem("e_ut"), 2 * c - 1 + m + 2 * EU * i)
                        pe.matmul(bank[b][:], w1_sb[:, 0, m * P:(m + 1) * P], h2t[:, c % 2, :], start=True, stop=False)
                        pe.matmul(bank[b][:], w1_sb[:, 1, m * P:(m + 1) * P], attr_mean[:, c % 2, :],
                                  start=False, stop=True).then_inc(sem("e_u_psum"), 1)
                c = k
                if edge(c):
                    layer0(c, 2, i)
                c = k - 1
                if edge(c):
                    pe.wait_ge(sem("e_ut"), 2 * (c + 1) + 2 * EU * i)
                    for j in range(TILES):
                        for m in range(2):
                            mm = pe.matmul(bank[0][:, j * P:(j + 1) * P], ut[:, c % 2, m, j * P:(j + 1) * P], w2_sb[:, m, :],
                                           start=(m == 0), stop=(m == 1))
                    mm.then_inc(sem("e_out_psum"), 1)
                c = k
                if edge(c):
                    layer0(c, 3, i)

            edge_pipeline(pe, edge_step)

        @block.scalar
        def _(act):
            act.wait_ge(sem("count_ready"), 1)
            act.activation(to_turn[0:ROWS, 3, :], count[0:ROWS, :], ACT.Ln, bias=1.0).then_inc(sem("amp_ready"), 1)
            act.wait_ge(sem("eps_ready"), 1)

            def node_step(k, i):
                c = k + 1
                if node(c):
                    pslot = c % 2
                    act.wait_ge(sem("n_turn1"), c + 1 + NU * i)
                    if c >= 2:
                        act.wait_ge(sem("n_y_psum"), c - 1 + NU * i)
                    act.activation(nht[:, pslot, :], bank[0][:], ACT.Relu).then_inc(sem("n_ht"), 1)
                c = k + 2
                if node(c):
                    act.wait_ge(sem("n_mv1"), c + 1 + NU * i)
                    if c >= 2:
                        act.wait_ge(sem("n_rs1"), c - 1 + NU * i)
                    act.activation(nsd1[:, c % 2, :], nmv1[:, c % 2, :, 1], ACT.Sqrt, bias=eps_col[:]).then_inc(sem("n_sd1"), 1)
                c = k
                if node(c):
                    act.wait_ge(sem("n_turn2"), c + 1 + NU * i)
                    if c >= 2:
                        act.wait_ge(sem("n_u_psum"), 2 * (c - 1) + 2 * NU * i)
                    act.activation(nh2t[:, c % 2, :], bank[2][:], ACT.Relu).then_inc(sem("n_h2t"), 1)
                    for m in range(2):
                        act.wait_ge(sem("n_u_psum"), 2 * c + m + 1 + 2 * NU * i)
                        if c >= 2:
                            act.wait_ge(sem("n_out_psum"), c - 1 + NU * i)
                        act.activation(nut[:, c % 2, m, :], bank[3 + m][:], ACT.Relu, bias=b1_col[:, m:m + 1]).then_inc(sem("n_ut"), 1)
                c = k + 1
                if node(c):
                    act.wait_ge(sem("n_mv2"), c + 1 + NU * i)
                    if c >= 2:
                        act.wait_ge(sem("n_rs2"), c - 1 + NU * i)
                    act.activation(nsd2[:, c % 2, :], nmv2[:, c % 2, :, 1], ACT.Sqrt, bias=eps_col[:]).then_inc(sem("n_sd2"), 1)

            node_pipeline(act, node_step)

            def edge_step(k, i):
                c = k + 1
                if edge(c):
                    act.wait_ge(sem("e_turned_s"), c + 1 + EU * i)
                    if c >= 2:
                        act.wait_ge(sem("e_b_psum"), c - 1 + EU * i)
                    act.activation(hst[:, c % 2, :], bank[0][:], ACT.Relu).then_inc(sem("e_hst"), 1)
                    act.wait_ge(sem("e_turned_d"), c + 1 + EU * i)
                    if c >= 2:
                        act.wait_ge(sem("e_layer0"), TILES * (c - 1) + TILES * EU * i)
                    act.activation(hdt[:, c % 2, :], bank[1][:], ACT.Relu).then_inc(sem("e_hdt"), 1)
                c = k + 2
                if edge(c):
                    act.wait_ge(sem("e_mv1"), c + 1 + EU * i)
                    if c >= 2:
                        act.wait_ge(sem("e_rs1"), c - 1 + EU * i)
                    act.activation(sd1[:, c % 2, :], mv1[:, c % 2, :, 1], ACT.Sqrt, bias=eps_col[:]).then_inc(sem("e_sd1"), 1)
                c = k - 1
                if edge(c):
                    act.wait_ge(sem("e_turned2"), c + 1 + EU * i)
                    if c >= 2:
                        act.wait_ge(sem("e_u_psum"), 2 * (c - 1) + 2 * EU * i)
                    act.activation(h2t[:, c % 2, :], bank[0][:], ACT.Relu).then_inc(sem("e_h2t"), 1)
                c = k + 1
                if edge(c):
                    act.wait_ge(sem("e_b_psum"), c + 1 + EU * i)
                    if c >= 2:
                        act.wait_ge(sem("e_sqsum"), c - 1 + EU * i)
                    act.activation(bsq[:, c % 2, :], bank[3][:], ACT.Square).then_inc(sem("e_bsq"), 1)
                c = k - 1
                if edge(c):
                    for m, b in ((0, 7), (1, 1)):
                        act.wait_ge(sem("e_u_psum"), 2 * c + m + 1 + 2 * EU * i)
                        if c >= 2:
                            act.wait_ge(sem("e_out_psum"), c - 1 + EU * i)
                        act.activation(ut[:, c % 2, m, :], bank[b][:], ACT.Relu, bias=b1_col[:, m:m + 1]).then_inc(sem("e_ut"), 1)
                c = k + 1
                if edge(c):
                    act.wait_ge(sem("e_mean_b"), c + 1 + EU * i)
                    if c >= 1:
                        act.wait_ge(sem("e_var"), c + EU * i)
                    act.activation(mean_b2[:], mean_b[:], ACT.Square).then_inc(sem("e_mean_b2"), 1)
                    act.wait_ge(sem("e_var"), c + 1 + EU * i)
                    if c >= 1:
                        act.wait_ge(sem(f"e_agg{SD}"), c + EU * i)
                    act.activation(var_pos[:], var[:], ACT.Relu).then_inc(sem("e_var_pos"), 1)
                    act.wait_ge(sem("e_var_pos"), c + 1 + EU * i)
                    if c >= 2:
                        act.wait_ge(sem("e_layer0"), TILES * (c - 1) + TILES * EU * i)
                    act.activation(agg[:, c % 2, SD, :], var_pos[:], ACT.Sqrt, bias=eps_col[:]).then_inc(sem(f"e_agg{SD}"), 1)
                c = k
                if edge(c):
                    act.wait_ge(sem("e_mv2"), c + 1 + EU * i)
                    if c >= 2:
                        act.wait_ge(sem("e_rs2"), c - 1 + EU * i)
                    act.activation(sd2[:, c % 2, :], mv2[:, c % 2, :, 1], ACT.Sqrt, bias=eps_col[:]).then_inc(sem("e_sd2"), 1)

            edge_pipeline(act, edge_step)

        @block.vector
        def _(dve):
            chain = sem("dve_setup")
            done = [0]

            def after(ins):
                ins.then_inc(chain, 1)
                done[0] += 1
                dve.wait_ge(chain, done[0])

            dve.memset(dst_i[:], FAR)
            dve.memset(src_i[:], 0).then_inc(sem("pad_written"), 1)
            dve.memset(eps_col[:], LN_EPS).then_inc(sem("eps_ready"), 1)
            log2 = math.log(2.0)
            for s, v in enumerate((1.0, log2, 1.0 / log2)):
                last = dve.memset(lone_std[:, s, :], math.sqrt(STD_EPS) * v)
            last.then_inc(sem("lone_std_ready"), 1)
            dve.wait_ge(sem("weights_turned"), 1)
            dve.tensor_copy(w_lin_t[:], bank[0][:, 0:P])
            dve.tensor_copy(wd_t[:], bank[0][:, P:2 * P])
            dve.tensor_copy(ws_t[:], bank[0][:, 2 * P:3 * P]).then_inc(sem("weights_copied"), 1)
            dve.wait_ge(sem("weights_in"), 16 * 13)
            dve.tensor_copy(b_post_wide[:], b_post_col[:].to_broadcast([P, P])).then_inc(sem("b_post_ready"), 1)
            dve.wait_ge(sem("comb_ready"), 1)
            dve.tensor_copy(comb_x[:], bank[1][:, 0:P])
            for b in range(1, 13):
                s, a = (b - 1) // AGGS, (b - 1) % AGGS
                last = dve.tensor_copy(comb_agg[:, a, s, :], bank[1 + b // 4][:, b % 4 * P:(b % 4 + 1) * P])
            last.then_inc(sem("comb_copied"), 1)
            dve.wait_ge(sem("const_psum"), 1)
            for j in range(TILES):
                last = dve.tensor_tensor(edge_const[:, j, :], bank[5][:, 0:P], b_lin_all[:], ALU.add)
                last.then_inc(sem("const_ready"), 1)
            dve.wait_ge(sem("const_ready"), TILES)
            dve.wait_ge(sem("const_psum"), 2)
            for j in range(TILES):
                last = dve.tensor_tensor(lone_const[:, j, :], bank[6][:, 0:P], edge_const[:, j, :], ALU.add)
                last.then_inc(sem("const_ready"), 1)

            R = slice(0, ROWS)
            dve.wait_ge(sem("edge_list_in"), 16 * 5)
            dve.wait_ge(sem("pos_ready"), 1)
            dve.tensor_copy(pos1[R], pos_i[R])
            dve.tensor_copy(to_turn[R, 0, :], src_i[R]).then_inc(sem("to_turn_ready"), 1)
            after(dve.tensor_copy(dst_f[R], dst_i[R]))
            dve.tensor_scalar(to_turn[R, 1, :], dst_f[R, 1:RW + 1], float(N - 1), None, ALU.min).then_inc(sem("to_turn_ready"), 1)
            dve.tensor_tensor(first[R], dst_f[R, 1:RW + 1], dst_f[R, 0:RW], ALU.not_equal)
            after(dve.tensor_tensor(final[R], dst_f[R, 1:RW + 1], dst_f[R, 2:RW + 2], ALU.not_equal))
            dve.tensor_scalar(keep_sb[R], first[R], -1.0, 1.0, ALU.mult, ALU.add)
            dve.tensor_scalar(reset_sb[R], first[R], RESET, None, ALU.mult)
            dve.tensor_scalar(lift_sb[R], first[R], -RESET, None, ALU.mult)
            after(dve.tensor_tensor(start_mark[R], first[R], pos1[R], ALU.mult))
            dve.tensor_tensor_scan(start_scan[R], start_mark[R], start_mark[R], 0.0, ALU.max, ALU.max).then_inc(sem("start_scanned"), 1)
            after(dve.tensor_scalar(far_sb[R], pos1[R], float(FAR), None, ALU.add))
            after(dve.tensor_tensor(far_diff[R], dst_f[R, 1:RW + 1], far_sb[R], ALU.subtract))
            after(dve.tensor_tensor(far_pick[R], far_diff[R], final[R], ALU.mult))
            dve.tensor_tensor(to_turn[R, 2, :], far_pick[R], far_sb[R], ALU.add).then_inc(sem("to_turn_ready"), 1)
            dve.memset(row_carry[:], 0.0)
            dve.wait_ge(sem("row_max_psum"), 1)
            after(dve.tensor_copy(row_max[0:1, R], bank[7][0:1, 0:ROWS]))
            dve.tensor_tensor_scan(row_carry[0:1, 1:ROWS], row_max[0:1, 0:ROWS - 1], row_max[0:1, 0:ROWS - 1], 0.0,
                                   ALU.max, ALU.max).then_inc(sem("row_carry_ready"), 1)
            dve.wait_ge(sem("carry_psum"), 1)
            after(dve.tensor_copy(carry_col[R], bank[7][0:ROWS, P:P + 1]))
            after(dve.tensor_scalar(seg_start[R], start_scan[R], carry_col[R], None, ALU.max))
            dve.scalar_tensor_tensor(count[R], pos1[R], 1.0, seg_start[R], ALU.add, ALU.subtract).then_inc(sem("count_ready"), 1)
            dve.wait_ge(sem("count_ready"), 1)
            dve.reciprocal(inv_count[R], count[R]).then_inc(sem("masks_done"), 1)
            dve.wait_ge(sem("amp_ready"), 1)
            dve.reciprocal(to_turn[R, 4, :], to_turn[R, 3, :]).then_inc(sem("to_turn_ready"), 2)
            for n in range(5):
                for h in range(2):
                    dve.wait_ge(sem("turned"), 2 * n + h + 1)
                    to = index[:, n, :, h] if n < 3 else scale[:, n - 3, :, h]
                    dve.tensor_copy(to, bank[h][:, 0:ROWS]).then_inc(sem("turned_out"), 1)

            def node_step(k, i):
                if node(k + 2):
                    c, b = k + 2, k % 2
                    dve.wait_ge(sem(f"n_in{b}"), 16 * (c // 2 + 1) + 16 * i)
                    for j in range(TILES):
                        last = dve.bn_stats(nbn1[:, b, j, :], nx[:, b, j, :])
                    last.then_inc(sem("n_bn1"), 1)
                    dve.wait_ge(sem("n_bn1"), c + 1 + NU * i)
                if node(k):
                    c, b = k, k % 2
                    dve.wait_ge(sem("n_sd2"), c + 1 + NU * i)
                    dve.reciprocal(nrs2[:, b, :], nsd2[:, b, :]).then_inc(sem("n_rs2"), 1)
                if node(k + 2):
                    b = k % 2
                    for j in range(TILES):
                        last = dve.bn_aggr(nmv1[:, b, j, :], nbn1[:, b, j, :])
                    last.then_inc(sem("n_mv1"), 1)
                if node(k):
                    c, b = k, k % 2
                    dve.wait_ge(sem("n_rs2"), c + 1 + NU * i)
                    if c >= 2:
                        dve.wait_ge(sem("n_turn2"), c - 1 + NU * i)
                    for j in range(TILES):
                        last = dve.tensor_scalar(nh2[:, b, j, :], nx1[:, b, j, :], nmv2[:, b, j, 0:1], nrs2[:, b, j:j + 1],
                                                 ALU.subtract, ALU.mult)
                    last.then_inc(sem("n_norm2"), 1)
                if node(k + 2):
                    c, b = k + 2, k % 2
                    dve.wait_ge(sem("n_sd1"), c + 1 + NU * i)
                    dve.reciprocal(nrs1[:, b, :], nsd1[:, b, :]).then_inc(sem("n_rs1"), 1)
                    dve.wait_ge(sem("n_rs1"), c + 1 + NU * i)
                    if c >= 2:
                        dve.wait_ge(sem("n_turn1"), c - 1 + NU * i)
                    for j in range(TILES):
                        last = dve.tensor_scalar(nh[:, b, j, :], nx[:, b, j, :], nmv1[:, b, j, 0:1], nrs1[:, b, j:j + 1],
                                                 ALU.subtract, ALU.mult)
                    last.then_inc(sem("n_norm1"), 1)
                if node(k + 1):
                    c, b = k + 1, (k + 1) % 2
                    dve.wait_ge(sem("n_y_psum"), c + 1 + NU * i)
                    dve.wait_ge(sem("n_xc"), c + 1 + NU * i)
                    if c >= 2:
                        dve.wait_ge(sem("n_x1b"), c - 1 + NU * i)
                        dve.wait_ge(sem("n_norm2"), c - 1 + NU * i)
                    dve.tensor_tensor(nx1[:, b], bank[1][:].rearrange("p (j f) -> p j f", j=TILES), nxc[:, b],
                                      ALU.add).then_inc(sem("n_x1"), 1)
                    dve.wait_ge(sem("n_x1"), c + 1 + NU * i)
                    for j in range(TILES):
                        last = dve.bn_stats(nbn2[:, b, j, :], nx1[:, b, j, :])
                    last.then_inc(sem("n_bn2"), 1)
                    dve.wait_ge(sem("n_bn2"), c + 1 + NU * i)
                if node(k - 1):
                    c, b = k - 1, (k - 1) % 2
                    dve.wait_ge(sem("n_out_psum"), c + 1 + NU * i)
                    dve.wait_ge(sem("n_x1b"), c + 1 + NU * i)
                    if c >= 2:
                        dve.wait_ge(sem(f"n_stored{b}"), 16 * (c // 2) + 16 * i)
                    dve.tensor_tensor(nout[:, b], bank[5][:].rearrange("p (j f) -> p j f", j=TILES), nx1b[:, b],
                                      ALU.add).then_inc(sem("n_out"), 1)
                if node(k + 1):
                    b = (k + 1) % 2
                    for j in range(TILES):
                        last = dve.bn_aggr(nmv2[:, b, j, :], nbn2[:, b, j, :])
                    last.then_inc(sem("n_mv2"), 1)

            node_pipeline(dve, node_step)

            def mix(c, j, i):
                b = c % 2
                acc = bank[5 + j % 2]
                dve.wait_ge(sem("e_layer0"), TILES * c + j + 1 + TILES * EU * i)
                if j == 0:
                    dve.wait_ge(sem("e_xdc"), c + 1 + EU * i)
                    dve.wait_ge(sem("e_scale"), c + 1 + EU * i)
                    if c >= 2:
                        dve.wait_ge(sem("e_x1b"), c - 1 + EU * i)
                        dve.wait_ge(sem("e_norm2"), c - 1 + EU * i)
                dve.scalar_tensor_tensor(part[:, j % 2, :], acc[:, P:2 * P], amp_att[:, c % 4, 0, j:j + 1], xdc[:, c % 4, j, :],
                                         ALU.mult, ALU.add).then_inc(sem("e_part"), 1)
                dve.wait_ge(sem("e_part"), TILES * c + j + 1 + TILES * EU * i)
                dve.scalar_tensor_tensor(part2[:, j % 2, :], acc[:, 2 * P:3 * P], amp_att[:, c % 4, 1, j:j + 1], part[:, j % 2, :],
                                         ALU.mult, ALU.add).then_inc(sem("e_part2"), 1)
                dve.wait_ge(sem("e_part2"), TILES * c + j + 1 + TILES * EU * i)
                ins = dve.tensor_tensor(x1[:, b, j, :], acc[:, 0:P], part2[:, j % 2, :], ALU.add)
                ins.then_inc(sem("e_mixed"), 1)

            def edge_step(k, i):
                if edge(k + 2):
                    c, b, s = k + 2, k % 2, (k + 2) % 4
                    dve.wait_ge(sem(f"e_gathered{s}"), 16 * 2 * TILES * (c // 4 + 1) + 16 * 2 * TILES * i)
                    for n, rows in ((0, xs), (1, xd)):
                        for j in range(TILES):
                            last = dve.bn_stats(bn1[:, b, n * TILES + j, :], rows[:, s, j, :])
                    last.then_inc(sem("e_bn1"), 1)
                    dve.wait_ge(sem("e_bn1"), c + 1 + EU * i)
                if edge(k - 1):
                    c, b = k - 1, (k - 1) % 2
                    dve.wait_ge(sem("e_sd2"), c + 1 + EU * i)
                    dve.reciprocal(rs2[:, b, :], sd2[:, b, :]).then_inc(sem("e_rs2"), 1)
                if edge(k + 2):
                    b = k % 2
                    for j in range(2 * TILES):
                        last = dve.bn_aggr(mv1[:, b, j, :], bn1[:, b, j, :])
                    last.then_inc(sem("e_mv1"), 1)
                if edge(k - 1):
                    c, b = k - 1, (k - 1) % 2
                    dve.wait_ge(sem("e_rs2"), c + 1 + EU * i)
                    if c >= 2:
                        dve.wait_ge(sem("e_turned2"), c - 1 + EU * i)
                    for j in range(TILES):
                        last = dve.tensor_scalar(h2[:, b, j, :], x1[:, b, j, :], mv2[:, b, j, 0:1], rs2[:, b, j:j + 1],
                                                 ALU.subtract, ALU.mult)
                    last.then_inc(sem("e_norm2"), 1)
                c = k + 2
                if edge(c):
                    b, s = c % 2, c % 4
                    dve.wait_ge(sem("e_sd1"), c + 1 + EU * i)
                    dve.reciprocal(rs1[:, b, :], sd1[:, b, :]).then_inc(sem("e_rs1"), 1)
                    dve.wait_ge(sem("e_rs1"), c + 1 + EU * i)
                    if c >= 2:
                        dve.wait_ge(sem("e_turned_d"), c - 1 + EU * i)
                    for n, rows, to in ((0, xs, hs), (1, xd, hd)):
                        for j in range(TILES):
                            m = n * TILES + j
                            last = dve.tensor_scalar(to[:, b, j, :], rows[:, s, j, :], mv1[:, b, m, 0:1], rs1[:, b, m:m + 1],
                                                     ALU.subtract, ALU.mult)
                    last.then_inc(sem("e_norm1"), 1)
                c = k
                if edge(c):
                    b, s = c % 2, c % 4
                    dve.wait_ge(sem(f"e_masks_in{s}"), 64 * (c // 4 + 1) + 64 * i)
                    dve.wait_ge(sem("e_turned_attr"), c + 1 + EU * i)
                    before = run_attr[:, 1 - b, CHUNK - 1:CHUNK] if c else 0.0
                    dve.tensor_tensor_scan(run_attr[:, b, :], keep[:, s, :], bank[2][:], before,
                                           ALU.mult, ALU.add).then_inc(sem("e_attr_run"), 1)
                    dve.wait_ge(sem("e_attr_run"), c + 1 + EU * i)
                    if c >= 2:
                        dve.wait_ge(sem("e_u_psum"), 2 * (c - 1) + 2 * EU * i)
                    dve.tensor_tensor(attr_mean[:, b, :], run_attr[:, b, :], inv[:, s, :], ALU.mult).then_inc(sem("e_attr_mean"), 1)
                c = k + 1
                if edge(c):
                    b, s = c % 2, c % 4
                    dve.wait_ge(sem("e_bsq"), c + 1 + EU * i)
                    dve.wait_ge(sem(f"e_masks_in{s}"), 64 * (c // 4 + 1) + 64 * i)
                    if c:
                        dve.wait_ge(sem("e_sqsum"), c + EU * i)
                    end = slice(CHUNK - 1, CHUNK)
                    dve.tensor_tensor_scan(run_max[:, b, :], reset[:, s, :], bank[3][:],
                                           run_max[:, 1 - b, end] if c else 0.0, ALU.add, ALU.max).then_inc(sem("e_max"), 1)
                    dve.tensor_tensor_scan(run_min[:, b, :], lift[:, s, :], bank[3][:],
                                           run_min[:, 1 - b, end] if c else 0.0, ALU.add, ALU.min).then_inc(sem("e_min"), 1)
                if edge(k):
                    mix(k, 0, i)
                if edge(c):
                    dve.tensor_tensor_scan(run_sum[:, b, :], keep[:, s, :], bank[3][:],
                                           run_sum[:, 1 - b, end] if c else 0.0, ALU.mult, ALU.add).then_inc(sem("e_sum"), 1)
                    dve.tensor_tensor_scan(run_sq[:, b, :], keep[:, s, :], bsq[:, b, :],
                                           run_sq[:, 1 - b, end] if c else 0.0, ALU.mult, ALU.add).then_inc(sem("e_sqsum"), 1)
                if edge(k):
                    mix(k, 1, i)
                if edge(c):
                    dve.wait_ge(sem("e_a_psum"), c + 1 + EU * i)
                    dve.wait_ge(sem("e_sum"), c + 1 + EU * i)
                    dve.wait_ge(sem("e_max"), c + 1 + EU * i)
                    dve.wait_ge(sem("e_min"), c + 1 + EU * i)
                    if c >= 2:
                        dve.wait_ge(sem("e_layer0"), TILES * (c - 1) + TILES * EU * i)
                    if c >= 1:
                        dve.wait_ge(sem("e_mean_b2"), c + EU * i)
                    dve.tensor_tensor(mean_b[:], run_sum[:, b, :], inv[:, s, :], ALU.mult).then_inc(sem("e_mean_b"), 1)
                    dve.scalar_tensor_tensor(agg[:, b, MX, :], bank[4][:], b_pre_col[:], run_max[:, b, :],
                                             ALU.add, ALU.add).then_inc(sem(f"e_agg{MX}"), 1)
                    dve.scalar_tensor_tensor(agg[:, b, MN, :], bank[4][:], b_pre_col[:], run_min[:, b, :],
                                             ALU.add, ALU.add).then_inc(sem(f"e_agg{MN}"), 1)
                if edge(k):
                    mix(k, 2, i)
                if edge(c):
                    dve.wait_ge(sem("e_sqsum"), c + 1 + EU * i)
                    dve.tensor_tensor(sq_mean[:], run_sq[:, b, :], inv[:, s, :], ALU.mult).then_inc(sem("e_sq_mean"), 1)
                    dve.wait_ge(sem("e_mean_b"), c + 1 + EU * i)
                    dve.scalar_tensor_tensor(agg[:, b, ME, :], bank[4][:], b_pre_col[:], mean_b[:],
                                             ALU.add, ALU.add).then_inc(sem(f"e_agg{ME}"), 1)
                    dve.wait_ge(sem("e_sq_mean"), c + 1 + EU * i)
                    dve.wait_ge(sem("e_mean_b2"), c + 1 + EU * i)
                    if c >= 1:
                        dve.wait_ge(sem("e_var_pos"), c + EU * i)
                    dve.tensor_tensor(var[:], sq_mean[:], mean_b2[:], ALU.subtract).then_inc(sem("e_var"), 1)
                    dve.wait_ge(sem("e_var"), c + 1 + EU * i)
                    dve.wait_ge(sem(f"e_agg{ME}"), c + 1 + EU * i)
                if edge(k):
                    c, b = k, k % 2
                    mix(c, 3, i)
                    dve.wait_ge(sem("e_mixed"), TILES * (c + 1) + TILES * EU * i)
                    for j in range(TILES):
                        last = dve.bn_stats(bn2[:, b, j, :], x1[:, b, j, :])
                    last.then_inc(sem("e_bn2"), 1)
                    dve.wait_ge(sem("e_bn2"), c + 1 + EU * i)
                if edge(k - 1):
                    c, b = k - 1, (k - 1) % 2
                    dve.wait_ge(sem("e_out_psum"), c + 1 + EU * i)
                    dve.wait_ge(sem("e_x1b"), c + 1 + EU * i)
                    if c == 0:
                        for n in range(2):
                            dve.wait_ge(sem(f"n_stored{n}"), 16 * ((NODE_CHUNKS - n + 1) // 2))
                    if c >= 2:
                        dve.wait_ge(sem(f"e_scattered{(c - 2) % 4}"), 16 * TILES * ((c - 2) // 4 + 1) + 16 * TILES * i)
                    dve.tensor_tensor(eout[:, b], bank[0][:].rearrange("p (j f) -> p j f", j=TILES), x1b[:, b],
                                      ALU.add).then_inc(sem("e_out"), 1)
                if edge(k):
                    b = k % 2
                    for j in range(TILES):
                        last = dve.bn_aggr(mv2[:, b, j, :], bn2[:, b, j, :])
                    last.then_inc(sem("e_mv2"), 1)

            edge_pipeline(dve, edge_step)


_NAMES = ["x", "src", "dst", "edge_attr_128", "L0_gnn_W_pre", "L0_gnn_b_pre", "L0_gnn_W_post", "L0_gnn_b_post",
          "L0_gnn_W_lin", "L0_gnn_b_lin", "L1_gnn_W1", "L1_gnn_b1", "L1_gnn_W2", "L1_gnn_b2"]


def kernel(**inputs):
    import numpy as np
    import concourse.bacc as bacc
    from concourse.bass_utils import run_bass_kernel_spmd

    nc = bacc.Bacc("TRN2", target_bir_lowering=False, num_devices=1)
    arrays, args = {}, []
    for name in _NAMES:
        a = np.ascontiguousarray(inputs[name])
        arrays[f"in_{name}"] = a
        args.append(nc.dram_tensor(f"in_{name}", a.shape, mybir.dt.from_np(a.dtype), kind="ExternalInput").ap())
    y = nc.dram_tensor("y", arrays["in_x"].shape, mybir.dt.float32, kind="ExternalOutput").ap()
    build(nc, *args, y)
    r = run_bass_kernel_spmd(nc, [arrays], core_ids=[0])
    return r.results[0]["y"]
```

```python
import math

import concourse.bass as bass
from concourse import mybir

ALU = mybir.AluOpType
ACT = mybir.ActivationFunctionType
F32 = mybir.dt.float32
BF16 = mybir.dt.bfloat16
I32 = mybir.dt.int32

P = 128
TILES = 4
CHUNK = P * TILES
LN_EPS = 1e-5
STD_EPS = 1e-5
FAR = 1 << 20
RESET = -3.0e38
AGGS = 4
SCALERS = 3
MX, MN, ME, SD = range(AGGS)


def build(nc, x, src, dst, edge_attr, w_pre, b_pre, w_post, b_post, w_lin, b_lin, w1, b1, w2, b2, out):
    N, F = x.shape
    E = src.shape[0]
    HID = w1.shape[1]
    assert F == P and HID == 2 * P and N >= CHUNK and N < FAR
    NODE_CHUNKS = -(-N // CHUNK)
    EDGE_CHUNKS = -(-E // CHUNK)
    ROWS = 2 * EDGE_CHUNKS
    RW = 2 * P
    FULL_ROWS = E // RW
    REST = E - FULL_ROWS * RW
    assert ROWS <= P and FULL_ROWS == ROWS - 1 and REST > 0
    LAST_EDGE_ROWS = E - (EDGE_CHUNKS - 1) * CHUNK

    keep_row = nc.dram_tensor("keep_row", [ROWS * RW], BF16, kind="Internal").ap()
    reset_row = nc.dram_tensor("reset_row", [ROWS * RW], BF16, kind="Internal").ap()
    lift_row = nc.dram_tensor("lift_row", [ROWS * RW], BF16, kind="Internal").ap()
    inv_row = nc.dram_tensor("inv_row", [ROWS * RW], F32, kind="Internal").ap()

    def sb(name, shape, dt=F32):
        return nc.alloc_sbuf_tensor(name, shape, dt)

    bank = [nc.alloc_psum_tensor(f"bank{i}", [P, CHUNK], F32) for i in range(8)]
    sems = {}

    def sem(name):
        if name not in sems:
            sems[name] = nc.alloc_semaphore(name)
        return sems[name]

    ident = sb("ident", [P, P])
    w_pre_sb = sb("w_pre_sb", [P, 2 * P])
    attr = sb("attr", [P, 4, TILES, P])
    w_post_sb = attr[:].rearrange("p s j f -> p (s j f)")[:, 0:13 * P]
    w_lin_sb = sb("w_lin_sb", [P, P])
    w_lin_t = sb("w_lin_t", [P, P])
    wd_t = sb("wd_t", [P, P])
    ws_t = sb("ws_t", [P, P])
    comb_x = sb("comb_x", [P, P])
    comb_agg = sb("comb_agg", [P, AGGS, SCALERS, P])
    w1_sb = sb("w1_sb", [P, 2, HID])
    w2_sb = sb("w2_sb", [P, 2, P])
    b1_col = sb("b1_col", [P, 2])
    b_pre_col = sb("b_pre_col", [P, 1])
    b_post_col = sb("b_post_col", [P, 1])
    b_post_wide = sb("b_post_wide", [P, P])
    b_lin_all = sb("b_lin_all", [P, P])
    b2_all = sb("b2_all", [P, TILES, P])
    edge_const = sb("edge_const", [P, TILES, P])
    lone_const = sb("lone_const", [P, TILES, P])
    lone_std = sb("lone_std", [P, SCALERS, P])
    eps_col = sb("eps_col", [P, 1])

    dst_i = sb("dst_i", [P, RW + 2], I32)
    src_i = sb("src_i", [P, RW], I32)
    pos_i = sb("pos_i", [P, RW], I32)
    dst_f = sb("dst_f", [P, RW + 2])
    agg = sb("agg", [P, 2, AGGS, CHUNK])
    work = agg[:].rearrange("p b a (n w) -> p (b a n) w", w=RW)
    first = work[:, 0, :]
    final = work[:, 1, :]
    pos1 = work[:, 2, :]
    start_mark = work[:, 3, :]
    start_scan = work[:, 4, :]
    seg_start = work[:, 5, :]
    row_max = sb("row_max", [1, P])
    row_carry = sb("row_carry", [1, P])
    carry_col = sb("carry_col", [P, 1])
    count = work[:, 6, :]
    inv_count = sb("inv_count", [P, RW])
    keep_sb = sb("keep_sb", [P, RW], BF16)
    reset_sb = sb("reset_sb", [P, RW], BF16)
    lift_sb = sb("lift_sb", [P, RW], BF16)
    far_sb = work[:, 7, :]
    far_diff = work[:, 8, :]
    far_pick = work[:, 9, :]
    to_turn = work[:, 10:15, :]
    index = sb("index", [P, 3, ROWS, 2], I32)
    scale = sb("scale", [P, 2, ROWS, 2])

    nx = sb("nx", [P, 4, TILES, P])
    nh = sb("nh", [P, 2, TILES, P])
    nht = sb("nht", [P, 2, CHUNK])
    nx1 = sb("nx1", [P, 2, TILES, P])
    nx1b = sb("nx1b", [P, 4, TILES, P])
    nh2 = sb("nh2", [P, 2, TILES, P])
    nh2t = sb("nh2t", [P, 2, CHUNK])
    nut = sb("nut", [P, 2, 2, CHUNK])
    nout = sb("nout", [P, 2, TILES, P])
    nbn1 = sb("nbn1", [P, 2, TILES, 6])
    nmv1 = sb("nmv1", [P, 2, TILES, 2])
    nsd1 = sb("nsd1", [P, 2, TILES])
    nrs1 = sb("nrs1", [P, 2, TILES])
    nbn2 = sb("nbn2", [P, 2, TILES, 6])
    nmv2 = sb("nmv2", [P, 2, TILES, 2])
    nsd2 = sb("nsd2", [P, 2, TILES])
    nrs2 = sb("nrs2", [P, 2, TILES])
    nms2 = sb("nms2", [P, 2, TILES])

    xs = sb("xs", [P, 4, TILES, P])
    xd = sb("xd", [P, 4, TILES, P])
    xdc = sb("xdc", [P, 4, TILES, P])
    nxc = xdc[:, 2:4]
    keep = sb("keep", [P, 4, CHUNK], BF16)
    reset = sb("reset", [P, 4, CHUNK], BF16)
    lift = sb("lift", [P, 4, CHUNK], BF16)
    inv = sb("inv", [P, 4, CHUNK])
    idx = sb("idx", [P, 4, 2, TILES], I32)
    stats_go = sb("stats_go", [P, 1])
    gather_go = sb("gather_go", [P, 1])
    oidx = sb("oidx", [P, 4, TILES], I32)
    amp_att = sb("amp_att", [P, 4, 2, TILES])
    bn1 = sb("bn1", [P, 2, 2 * TILES, 6])
    mv1 = sb("mv1", [P, 2, 2 * TILES, 2])
    sd1 = sb("sd1", [P, 2, 2 * TILES])
    rs1 = sb("rs1", [P, 2, 2 * TILES])
    ms1 = sb("ms1", [P, 2, TILES])
    hs = sb("hs", [P, 2, TILES, P])
    hd = sb("hd", [P, 2, TILES, P])
    hst = sb("hst", [P, 2, CHUNK])
    hdt = sb("hdt", [P, 2, CHUNK])
    bsq = sb("bsq", [P, 2, CHUNK])
    run_max = sb("run_max", [P, 2, CHUNK])
    run_min = sb("run_min", [P, 2, CHUNK])
    run_sum = sb("run_sum", [P, 2, CHUNK])
    run_sq = sb("run_sq", [P, 2, CHUNK])
    run_attr = sb("run_attr", [P, 2, CHUNK])
    mean_b = sb("mean_b", [P, CHUNK])
    mean_b2 = sb("mean_b2", [P, CHUNK])
    sq_mean = sb("sq_mean", [P, CHUNK])
    var = sb("var", [P, CHUNK])
    var_pos = sb("var_pos", [P, CHUNK])
    attr_mean = sb("attr_mean", [P, 2, CHUNK])
    part = sb("part", [P, 2, P])
    part2 = sb("part2", [P, 2, P])
    x1 = nx1
    x1b = nx1b
    bn2 = sb("bn2", [P, 2, TILES, 6])
    mv2 = sb("mv2", [P, 2, TILES, 2])
    sd2 = sb("sd2", [P, 2, TILES])
    rs2 = sb("rs2", [P, 2, TILES])
    ms2 = sb("ms2", [P, 2, TILES])
    h2 = nh2
    h2t = nh2t
    ut = nut
    eout = nout

    NU, EU = 4, 4
    N_LO, N_HI, N_LOOP = -6, NODE_CHUNKS + 2, 6
    N_LOOPS = (NODE_CHUNKS - 7 - N_LOOP) // NU
    E_LO, E_HI, E_LOOP = -4, EDGE_CHUNKS + 2, 4
    E_LOOPS = (EDGE_CHUNKS - 5 - E_LOOP) // EU

    def run_passes(eng, node_step, edge_step):
        for k in range(N_LO, N_LOOP):
            node_step(k, 0)
        with eng.Fori(0, N_LOOPS) as i:
            for u in range(NU):
                node_step(N_LOOP + u, i)
        for k in range(N_LOOP + N_LOOPS * NU, N_HI):
            node_step(k, 0)
            if k - N_HI >= E_LO:
                edge_step(k - N_HI, 0)
        for k in range(0, E_LOOP):
            edge_step(k, 0)
        with eng.Fori(0, E_LOOPS) as i:
            for u in range(EU):
                edge_step(E_LOOP + u, i)
        for k in range(E_LOOP + E_LOOPS * EU, E_HI):
            edge_step(k, 0)

    def node(c):
        return 0 <= c < NODE_CHUNKS

    def edge(c):
        return 0 <= c < EDGE_CHUNKS

    def node_rows(ap, c, i):
        base = min(c * CHUNK, N - CHUNK) + i * (NU * CHUNK)
        return ap[bass.ds(base, CHUNK), :].rearrange("(p j) f -> p j f", j=TILES)

    with nc.Block() as block:

        @block.sync
        def _(sp):
            w = sem("weights_in")
            sp.dma_start(w_lin_sb[:], w_lin).then_inc(w, 16)
            sp.dma_start(w_pre_sb[:], w_pre).then_inc(w, 16)
            sp.dma_start(w_post_sb, w_post).then_inc(w, 16)
            sp.dma_start(w1_sb[:], w1.rearrange("(k p) h -> p k h", p=P)).then_inc(w, 16)
            sp.dma_start(w2_sb[:], w2.rearrange("(k p) h -> p k h", p=P)).then_inc(w, 16)
            sp.dma_start(b_lin_all[:], b_lin.rearrange("(a f) -> a f", a=1).to_broadcast([P, P])).then_inc(w, 16)
            for j in range(TILES):
                sp.dma_start(b2_all[:, j, :], b2.rearrange("(a f) -> a f", a=1).to_broadcast([P, P])).then_inc(w, 16)
            with nc.allow_non_contiguous_dma(reason="a bias as one value per partition"):
                sp.dma_start(b1_col[:], b1.rearrange("(k p) -> p k", p=P)).then_inc(w, 16)
                sp.dma_start(b_pre_col[:], b_pre.rearrange("(p a) -> p a", a=1)).then_inc(w, 16)
                sp.dma_start(b_post_col[:], b_post.rearrange("(p a) -> p a", a=1)).then_inc(w, 16)

            sp.wait_ge(sem("pad_written"), 1)
            e = sem("edge_list_in")
            d = dst.tensor
            sp.dma_start(dst_i[0:1, 1:RW + 2], bass.AP(tensor=d, offset=0, ap=[[RW + 1, 1], [1, RW + 1]])).then_inc(e, 16)
            sp.dma_start(dst_i[1:FULL_ROWS, :],
                         bass.AP(tensor=d, offset=RW - 1, ap=[[RW, FULL_ROWS - 1], [1, RW + 2]])).then_inc(e, 16)
            sp.dma_start(dst_i[FULL_ROWS:ROWS, 0:REST + 1],
                         bass.AP(tensor=d, offset=FULL_ROWS * RW - 1, ap=[[REST + 1, 1], [1, REST + 1]])).then_inc(e, 16)
            sp.dma_start(src_i[0:FULL_ROWS, :], src[0:FULL_ROWS * RW].rearrange("(r w) -> r w", w=RW)).then_inc(e, 16)
            sp.dma_start(src_i[FULL_ROWS:ROWS, 0:REST],
                         src[FULL_ROWS * RW:E].rearrange("(a w) -> a w", a=1)).then_inc(e, 16)

            sp.wait_ge(sem("masks_done"), 1)
            r = sem("rows_out")
            sp.dma_start(keep_row.rearrange("(r w) -> r w", w=RW), keep_sb[0:ROWS, :]).then_inc(r, 16)
            sp.dma_start(reset_row.rearrange("(r w) -> r w", w=RW), reset_sb[0:ROWS, :]).then_inc(r, 16)
            sp.dma_start(lift_row.rearrange("(r w) -> r w", w=RW), lift_sb[0:ROWS, :]).then_inc(r, 16)
            sp.dma_start(inv_row.rearrange("(r w) -> r w", w=RW), inv_count[0:ROWS, :]).then_inc(r, 16)

            def node_step(k, i):
                c = k + 6
                if node(c):
                    if c >= 4:
                        sp.wait_ge(sem("n_norm1"), c - 3 + NU * i)
                        sp.wait_ge(sem("n_xc"), c - 3 + NU * i)
                    sp.dma_start(nx[:, c % 4], node_rows(x, c, i)).then_inc(sem(f"n_in{c % 4}"), 16)
                c = k - 2
                if node(c):
                    sp.wait_ge(sem("n_out"), c + 1 + NU * i)
                    if c == NODE_CHUNKS - 1:
                        sp.wait_ge(sem(f"n_stored{(c - 1) % 2}"), 16 * ((c - 1) // 2 + 1))
                    sp.dma_start(node_rows(out, c, i), nout[:, c % 2]).then_inc(sem(f"n_stored{c % 2}"), 16)

            def edge_step(k, i):
                c = k + 4
                if edge(c):
                    s = c % 4
                    if c == 0:
                        sp.wait_ge(r, 64)
                    if c >= 4:
                        sp.wait_ge(sem("e_attr_mean"), c - 3 + EU * i)
                        sp.wait_ge(sem("e_turned_attr"), c - 3 + EU * i)
                    m = sem(f"e_masks_in{s}")
                    for dst_sb, row in ((keep, keep_row), (reset, reset_row), (lift, lift_row), (inv, inv_row)):
                        sp.dma_start(dst_sb[:, s, :],
                                     row[bass.ds(c * CHUNK + i * (EU * CHUNK), CHUNK)]
                                     .rearrange("(a w) -> a w", a=1).to_broadcast([P, CHUNK])).then_inc(m, 16)
                    a = sem(f"e_attr_in{s}")
                    if c < EDGE_CHUNKS - 1:
                        rows = edge_attr[bass.ds(c * CHUNK + i * (EU * CHUNK), CHUNK), :]
                        sp.dma_start(attr[:, s], rows.rearrange("(j p) f -> p j f", p=P)).then_inc(a, 16)
                    else:
                        whole = LAST_EDGE_ROWS // P
                        base = c * CHUNK
                        sp.dma_start(attr[:, s, 0:whole, :],
                                     edge_attr[base:base + whole * P, :].rearrange("(j p) f -> p j f", p=P)).then_inc(a, 16)
                        sp.dma_start(attr[0:LAST_EDGE_ROWS - whole * P, s, whole, :],
                                     edge_attr[base + whole * P:E, :]).then_inc(a, 16)

            run_passes(sp, node_step, edge_step)

        @block.gpsimd
        def _(pool):
            fixed = sem("ident_ready")
            pool.memset(ident[:], 0.0).then_inc(sem("ident_zero"), 1)
            pool.iota(pos_i[:], pattern=[[1, RW]], base=1, channel_multiplier=RW).then_inc(sem("pos_ready"), 1)
            pool.wait_ge(sem("ident_zero"), 1)
            pool.affine_select(out=ident[:], in_=ident[:], compare_op=ALU.not_equal, fill=1.0, base=0,
                               pattern=[[-1, P]], channel_multiplier=1).then_inc(sem("ident_ready"), 1)
            pool.wait_ge(sem("const_ready"), 2 * TILES)

            def node_step(k, i):
                c = k
                if node(c):
                    pool.wait_ge(sem("n_x1"), c + 1 + NU * i)
                    if c >= 4:
                        pool.wait_ge(sem("n_out"), c - 3 + NU * i)
                    if c == 0:
                        pool.wait_ge(sem("weights_in"), 16 * 13)
                    pool.tensor_tensor(nx1b[:, c % 4], nx1[:, c % 2], b2_all[:], ALU.add).then_inc(sem("n_x1b"), 1)
                c = k + 2
                if node(c):
                    pool.wait_ge(sem(f"n_in{c % 4}"), 16 * (c // 4 + 1) + 16 * i)
                    if c >= 2:
                        pool.wait_ge(sem("n_x1"), c - 1 + NU * i)
                    pool.tensor_tensor(nxc[:, c % 2], nx[:, c % 4], lone_const[:], ALU.add).then_inc(sem("n_xc"), 1)

            def edge_step(k, i):
                c = k - 1
                if edge(c):
                    pool.wait_ge(sem("e_mixed"), TILES * (c + 1) + TILES * EU * i)
                    if c >= 4:
                        pool.wait_ge(sem("e_out"), c - 3 + EU * i)
                    if c == 0:
                        pool.wait_ge(sem("n_out"), NODE_CHUNKS)
                    pool.tensor_tensor(x1b[:, c % 4], x1[:, c % 2], b2_all[:], ALU.add).then_inc(sem("e_x1b"), 1)
                c = k + 2
                if edge(c):
                    pool.wait_ge(sem(f"e_gathered{c % 4}"), 16 * 2 * TILES * (c // 4 + 1) + 16 * 2 * TILES * i)
                    if c == 2:
                        pool.wait_ge(sem("n_x1"), NODE_CHUNKS)
                    if c >= 4:
                        pool.wait_ge(sem("e_mixed"), TILES * (c - 3) + TILES * EU * i)
                    pool.tensor_tensor(xdc[:, c % 4], xd[:, c % 4], edge_const[:], ALU.add).then_inc(sem("e_xdc"), 1)
                    t = bass.ds(2 * c + (2 * EU) * i, 2)
                    pool.tensor_copy(amp_att[:, c % 4].rearrange("p w (r h) -> p w r h", h=2), scale[:, :, t, :]).then_inc(sem("e_scale"), 1)
                c = k - 2
                if edge(c):
                    pool.wait_ge(fixed, 1)
                    pool.wait_ge(sem("e_out"), c + 1 + EU * i)
                    if c == 0:
                        for n in range(2):
                            pool.wait_ge(sem(f"n_stored{n}"), 16 * ((NODE_CHUNKS - n + 1) // 2))
                    if c >= 4:
                        pool.wait_ge(sem(f"e_scattered{c % 4}"), 16 * TILES * (c // 4) + 16 * TILES * i)
                    t = bass.ds(2 * c + (2 * EU) * i, 2)
                    pool.tensor_copy(oidx[:, c % 4].rearrange("p (r h) -> p r h", h=2), index[:, 2, t, :]).then_inc(sem("e_oidx"), 1)
                c = k + 4
                if edge(c):
                    s = c % 4
                    pool.wait_ge(fixed, 1)
                    if c == 0:
                        pool.wait_ge(sem("turned_out"), 10)
                    if c >= 4:
                        pool.wait_ge(sem(f"e_gathered{s}"), 16 * 2 * TILES * (c // 4) + 16 * 2 * TILES * i)
                        pool.wait_ge(sem("e_norm1"), c - 3 + EU * i)
                        pool.wait_ge(sem("e_norm1d"), c - 3 + EU * i)
                        pool.wait_ge(sem("e_xdc"), c - 3 + EU * i)
                    t = bass.ds(2 * c + (2 * EU) * i, 2)
                    pool.tensor_copy(idx[:, s].rearrange("p w (r h) -> p w r h", h=2), index[:, 0:2, t, :]).then_inc(sem("e_idx"), 1)
                    pool.wait_ge(sem("e_idx"), c + 1 + EU * i)
                    if edge(k - 2):
                        pool.wait_ge(sem("e_oidx"), k - 1 + EU * i)
                    pool.tensor_tensor(gather_go[:], eps_col[:], eps_col[:], ALU.add)
                    g = sem(f"e_gathered{s}")
                    for j in range(TILES):
                        for which, rows in ((0, xs), (1, xd)):
                            pool.indirect_dma_start(
                                out=rows[:, s, j, :], out_offset=None, in_=x,
                                in_offset=bass.IndirectOffsetOnAxis(ap=idx[:, s, which, j:j + 1], axis=0)).then_inc(g, 16)
                c = k - 2
                if edge(c):
                    if not edge(k + 4):
                        pool.wait_ge(sem("e_oidx"), k - 1)
                    for j in range(TILES):
                        pool.indirect_dma_start(
                            out=out, out_offset=bass.IndirectOffsetOnAxis(ap=oidx[:, c % 4, j:j + 1], axis=0),
                            in_=eout[:, c % 2, j, :], in_offset=None,
                            bounds_check=N - 1, oob_is_err=False).then_inc(sem(f"e_scattered{c % 4}"), 16)
                c = k
                if edge(c):
                    pool.wait_ge(sem("e_attr_run"), c + 1 + EU * i)
                    if c >= 2:
                        pool.wait_ge(sem("e_u_psum"), 2 * (c - 1) + 2 * EU * i)
                    if c < 4:
                        pool.wait_ge(sem(f"e_masks_in{c % 4}"), 64)
                    pool.tensor_tensor(attr_mean[:, c % 2, :], run_attr[:, c % 2, :], inv[:, c % 4, :],
                                       ALU.mult).then_inc(sem("e_attr_mean"), 1)

            run_passes(pool, node_step, edge_step)
            for s in range(4):
                pool.wait_ge(sem(f"e_scattered{s}"), 16 * TILES * ((EDGE_CHUNKS - s + 3) // 4))

        @block.tensor
        def _(pe):
            pe.wait_ge(sem("ident_ready"), 1)
            pe.wait_ge(sem("weights_in"), 16 * 13)
            pe.transpose(bank[0][:, 0:P], w_lin_sb[:], ident[:])
            pe.transpose(bank[0][:, P:2 * P], w_pre_sb[:, 0:P], ident[:])
            pe.transpose(bank[0][:, 2 * P:3 * P], w_pre_sb[:, P:2 * P], ident[:]).then_inc(sem("weights_turned"), 1)
            pe.wait_ge(sem("weights_copied"), 1)
            for b in range(13):
                mm = pe.matmul(bank[1 + b // 4][:, b % 4 * P:(b % 4 + 1) * P], w_post_sb[:, b * P:(b + 1) * P], w_lin_t[:],
                               start=True, stop=True)
            mm.then_inc(sem("comb_ready"), 1)
            pe.wait_ge(sem("b_post_ready"), 1)
            pe.matmul(bank[5][:, 0:P], b_post_wide[:], w_lin_t[:], start=True, stop=True).then_inc(sem("const_psum"), 1)
            pe.wait_ge(sem("comb_copied"), 1)
            pe.wait_ge(sem("lone_std_ready"), 1)
            for s in range(SCALERS):
                mm = pe.matmul(bank[6][:, 0:P], lone_std[:, s, :], comb_agg[:, SD, s, :], start=(s == 0), stop=(s == SCALERS - 1))
            mm.then_inc(sem("const_psum"), 1)
            pe.wait_ge(sem("start_scanned"), 1)
            pe.transpose(bank[7][0:1, 0:ROWS], start_scan[0:ROWS, RW - 1:RW], ident[0:ROWS, 0:ROWS]).then_inc(sem("row_max_psum"), 1)
            pe.wait_ge(sem("row_carry_ready"), 1)
            pe.transpose(bank[7][0:ROWS, P:P + 1], row_carry[0:1, 0:ROWS], ident[0:1, 0:1]).then_inc(sem("carry_psum"), 1)
            for n in range(5):
                pe.wait_ge(sem("to_turn_ready"), n + 1)
                for h in range(2):
                    if 2 * n + h >= 2:
                        pe.wait_ge(sem("turned_out"), 2 * n + h - 1)
                    pe.transpose(bank[h][:, 0:ROWS], to_turn[0:ROWS, n, h * P:(h + 1) * P],
                                 ident[0:ROWS, 0:ROWS]).then_inc(sem("turned"), 1)
            pe.wait_ge(sem("turned_out"), 10)

            def node_step(k, i):
                c = k + 1
                if node(c):
                    pe.wait_ge(sem("n_norm1"), c + 1 + NU * i)
                    if c >= 1:
                        pe.wait_ge(sem("n_ht"), c + NU * i)
                    for j in range(TILES):
                        mm = pe.transpose(bank[0][:, j * P:(j + 1) * P], nh[:, c % 2, j, :], ident[:])
                    mm.then_inc(sem("n_turn1"), 1)
                c = k - 1
                if node(c):
                    pe.wait_ge(sem("n_norm2"), c + 1 + NU * i)
                    if c >= 1:
                        pe.wait_ge(sem("n_h2t"), c + NU * i)
                    for j in range(TILES):
                        mm = pe.transpose(bank[2][:, j * P:(j + 1) * P], nh2[:, c % 2, j, :], ident[:])
                    mm.then_inc(sem("n_turn2"), 1)
                c = k - 2
                if node(c):
                    pe.wait_ge(sem("n_ut"), 2 * (c + 1) + 2 * NU * i)
                    if c >= 1:
                        pe.wait_ge(sem("n_out"), c + NU * i)
                    for j in range(TILES):
                        for m in range(2):
                            mm = pe.matmul(bank[5][:, j * P:(j + 1) * P], nut[:, c % 2, m, j * P:(j + 1) * P], w2_sb[:, m, :],
                                           start=(m == 0), stop=(m == 1))
                    mm.then_inc(sem("n_out_psum"), 1)
                c = k + 1
                if node(c):
                    pe.wait_ge(sem("n_ht"), c + 1 + NU * i)
                    if c >= 1:
                        pe.wait_ge(sem("n_x1"), c + NU * i)
                    for j in range(TILES):
                        mm = pe.matmul(bank[1][:, j * P:(j + 1) * P], nht[:, c % 2, j * P:(j + 1) * P], comb_x[:],
                                       start=True, stop=True)
                    mm.then_inc(sem("n_y_psum"), 1)
                c = k - 1
                if node(c):
                    pe.wait_ge(sem("n_h2t"), c + 1 + NU * i)
                    for m in range(2):
                        if c >= 1:
                            pe.wait_ge(sem("n_ut"), 2 * c - 1 + m + 2 * NU * i)
                        pe.matmul(bank[6 + m][:], w1_sb[:, 0, m * P:(m + 1) * P], nh2t[:, c % 2, :],
                                  start=True, stop=True).then_inc(sem("n_u_psum"), 1)

            def layer0(c, j, i):
                acc = bank[5 + j % 2]
                if c == 0 and j == 0:
                    pe.wait_ge(sem("n_out"), NODE_CHUNKS)
                if c == 0 and j == 1:
                    pe.wait_ge(sem("n_ut"), 2 * NODE_CHUNKS)
                if j >= 2:
                    pe.wait_ge(sem("e_mixed"), TILES * c + j - 1 + TILES * EU * i)
                elif c >= 1:
                    pe.wait_ge(sem("e_mixed"), TILES * (c - 1) + j + 3 + TILES * EU * i)
                cols = slice(j * P, (j + 1) * P)
                for a in range(AGGS):
                    if j == 0:
                        pe.wait_ge(sem(f"e_agg{a}"), c + 1 + EU * i)
                    pe.matmul(acc[:, 0:SCALERS * P], agg[:, c % 2, a, cols],
                              comb_agg[:, a].rearrange("p s f -> p (s f)"), start=(a == 0), stop=False,
                              skip_group_check=True)
                pe.matmul(acc[:, 0:P], hdt[:, c % 2, cols], comb_x[:], start=False, stop=True,
                          skip_group_check=True).then_inc(sem("e_layer0"), 1)

            def edge_step(k, i):
                c = k + 1
                if edge(c):
                    pe.wait_ge(sem("e_norm1"), c + 1 + EU * i)
                    if c == 0:
                        pe.wait_ge(sem("n_ht"), NODE_CHUNKS)
                        pe.wait_ge(sem("n_x1"), NODE_CHUNKS)
                    if c >= 3:
                        pe.wait_ge(sem("e_h2t"), c - 2 + EU * i)
                    for j in range(TILES):
                        mm = pe.transpose(bank[0][:, j * P:(j + 1) * P], hs[:, c % 2, j, :], ident[:])
                    mm.then_inc(sem("e_turned_s"), 1)
                    pe.wait_ge(sem("e_norm1d"), c + 1 + EU * i)
                    if c >= 3:
                        pe.wait_ge(sem("e_ut"), 2 * (c - 2) + 2 * EU * i)
                    for j in range(TILES):
                        mm = pe.transpose(bank[1][:, j * P:(j + 1) * P], hd[:, c % 2, j, :], ident[:])
                    mm.then_inc(sem("e_turned_d"), 1)
                c = k
                if edge(c):
                    pe.wait_ge(sem(f"e_attr_in{c % 4}"),
                               16 * (c // 4 + 1) + 16 * i + (16 if c == EDGE_CHUNKS - 1 else 0))
                    if c == 0:
                        pe.wait_ge(sem("n_h2t"), NODE_CHUNKS)
                    if c >= 1:
                        pe.wait_ge(sem("e_attr_run"), c + EU * i)
                    for j in range(TILES):
                        mm = pe.transpose(bank[2][:, j * P:(j + 1) * P], attr[:, c % 4, j, :], ident[:])
                    mm.then_inc(sem("e_turned_attr"), 1)
                    layer0(c, 0, i)
                c = k + 1
                if edge(c):
                    pe.wait_ge(sem("e_hst"), c + 1 + EU * i)
                    if c >= 1:
                        pe.wait_ge(sem("e_sum"), c + EU * i)
                        pe.wait_ge(sem("e_bsq"), c + EU * i)
                    pe.matmul(bank[3][:], ws_t[:], hst[:, c % 2, :], start=True, stop=True).then_inc(sem("e_b_psum"), 1)
                    pe.wait_ge(sem("e_hdt"), c + 1 + EU * i)
                    if c >= 1:
                        pe.wait_ge(sem(f"e_agg{ME}"), c + EU * i)
                    pe.matmul(bank[4][:], wd_t[:], hdt[:, c % 2, :], start=True, stop=True).then_inc(sem("e_a_psum"), 1)
                c = k - 1
                if edge(c):
                    pe.wait_ge(sem("e_norm2"), c + 1 + EU * i)
                    if not edge(k + 1) and c >= 1:
                        pe.wait_ge(sem("e_h2t"), c + EU * i)
                    for j in range(TILES):
                        mm = pe.transpose(bank[0][:, j * P:(j + 1) * P], h2[:, c % 2, j, :], ident[:])
                    mm.then_inc(sem("e_turned2"), 1)
                c = k
                if edge(c):
                    layer0(c, 1, i)
                c = k - 1
                if edge(c):
                    pe.wait_ge(sem("e_h2t"), c + 1 + EU * i)
                    pe.wait_ge(sem("e_attr_mean"), c + 1 + EU * i)
                    if c >= 1:
                        pe.wait_ge(sem("e_out"), c + EU * i)
                    for m, b in ((0, 7), (1, 1)):
                        if c >= 1:
                            pe.wait_ge(sem("e_ut"), 2 * c - 1 + m + 2 * EU * i)
                        pe.matmul(bank[b][:], w1_sb[:, 0, m * P:(m + 1) * P], h2t[:, c % 2, :], start=True, stop=False)
                        pe.matmul(bank[b][:], w1_sb[:, 1, m * P:(m + 1) * P], attr_mean[:, c % 2, :],
                                  start=False, stop=True).then_inc(sem("e_u_psum"), 1)
                c = k
                if edge(c):
                    layer0(c, 2, i)
                c = k - 1
                if edge(c):
                    pe.wait_ge(sem("e_ut"), 2 * (c + 1) + 2 * EU * i)
                    for j in range(TILES):
                        for m in range(2):
                            mm = pe.matmul(bank[7][:, j * P:(j + 1) * P], ut[:, c % 2, m, j * P:(j + 1) * P], w2_sb[:, m, :],
                                           start=(m == 0), stop=(m == 1))
                    mm.then_inc(sem("e_out_psum"), 1)
                c = k
                if edge(c):
                    layer0(c, 3, i)

            run_passes(pe, node_step, edge_step)

        @block.scalar
        def _(act):
            act.wait_ge(sem("count_ready"), 1)
            act.activation(to_turn[0:ROWS, 3, :], count[0:ROWS, :], ACT.Ln, bias=1.0).then_inc(sem("amp_ready"), 1)
            act.wait_ge(sem("eps_ready"), 1)

            def node_step(k, i):
                c = k
                if node(c):
                    act.wait_ge(sem("n_mv2"), c + 1 + NU * i)
                    if c >= 2:
                        act.wait_ge(sem("n_rs2"), c - 1 + NU * i)
                    act.activation(nsd2[:, c % 2, :], nmv2[:, c % 2, :, 1], ACT.Sqrt, bias=eps_col[:]).then_inc(sem("n_sd2"), 1)
                c = k + 1
                if node(c):
                    act.wait_ge(sem("n_turn1"), c + 1 + NU * i)
                    if c >= 2:
                        act.wait_ge(sem("n_y_psum"), c - 1 + NU * i)
                    act.activation(nht[:, c % 2, :], bank[0][:], ACT.Relu).then_inc(sem("n_ht"), 1)
                c = k - 1
                if node(c):
                    act.wait_ge(sem("n_turn2"), c + 1 + NU * i)
                    if c >= 2:
                        act.wait_ge(sem("n_u_psum"), 2 * (c - 1) + 2 * NU * i)
                    act.activation(nh2t[:, c % 2, :], bank[2][:], ACT.Relu).then_inc(sem("n_h2t"), 1)
                c = k + 3
                if node(c):
                    act.wait_ge(sem("n_mv1"), c + 1 + NU * i)
                    if c >= 2:
                        act.wait_ge(sem("n_rs1"), c - 1 + NU * i)
                    act.activation(nsd1[:, c % 2, :], nmv1[:, c % 2, :, 1], ACT.Sqrt, bias=eps_col[:]).then_inc(sem("n_sd1"), 1)
                c = k
                if node(c):
                    b = c % 2
                    act.wait_ge(sem("n_ms2"), c + 1 + NU * i)
                    if c >= 2:
                        act.wait_ge(sem("n_turn2"), c - 1 + NU * i)
                    for j in range(TILES):
                        last = act.activation(nh2[:, b, j, :], nx1[:, b, j, :], ACT.Identity,
                                              scale=nrs2[:, b, j:j + 1], bias=nms2[:, b, j:j + 1])
                    last.then_inc(sem("n_norm2"), 1)
                c = k - 1
                if node(c):
                    for m in range(2):
                        act.wait_ge(sem("n_u_psum"), 2 * c + m + 1 + 2 * NU * i)
                        if c >= 2:
                            act.wait_ge(sem("n_out_psum"), c - 1 + NU * i)
                        act.activation(nut[:, c % 2, m, :], bank[6 + m][:], ACT.Relu, bias=b1_col[:, m:m + 1]).then_inc(sem("n_ut"), 1)

            def edge_step(k, i):
                c = k - 1
                if edge(c):
                    act.wait_ge(sem("e_mv2"), c + 1 + EU * i)
                    if c >= 2:
                        act.wait_ge(sem("e_rs2"), c - 1 + EU * i)
                    act.activation(sd2[:, c % 2, :], mv2[:, c % 2, :, 1], ACT.Sqrt, bias=eps_col[:]).then_inc(sem("e_sd2"), 1)
                c = k + 1
                if edge(c):
                    act.wait_ge(sem("e_turned_s"), c + 1 + EU * i)
                    if c >= 2:
                        act.wait_ge(sem("e_b_psum"), c - 1 + EU * i)
                    act.activation(hst[:, c % 2, :], bank[0][:], ACT.Relu).then_inc(sem("e_hst"), 1)
                    act.wait_ge(sem("e_turned_d"), c + 1 + EU * i)
                    if c >= 2:
                        act.wait_ge(sem("e_layer0"), TILES * (c - 1) + TILES * EU * i)
                    act.activation(hdt[:, c % 2, :], bank[1][:], ACT.Relu).then_inc(sem("e_hdt"), 1)
                c = k - 1
                if edge(c):
                    b = c % 2
                    act.wait_ge(sem("e_ms2"), c + 1 + EU * i)
                    if c >= 2:
                        act.wait_ge(sem("e_turned2"), c - 1 + EU * i)
                    for j in range(TILES):
                        last = act.activation(h2[:, b, j, :], x1[:, b, j, :], ACT.Identity,
                                              scale=rs2[:, b, j:j + 1], bias=ms2[:, b, j:j + 1])
                    last.then_inc(sem("e_norm2"), 1)
                c = k + 2
                if edge(c):
                    act.wait_ge(sem("e_mv1"), c + 1 + EU * i)
                    if c >= 2:
                        act.wait_ge(sem("e_rs1"), c - 1 + EU * i)
                    act.activation(sd1[:, c % 2, :], mv1[:, c % 2, :, 1], ACT.Sqrt, bias=eps_col[:]).then_inc(sem("e_sd1"), 1)
                c = k + 1
                if edge(c):
                    act.wait_ge(sem("e_b_psum"), c + 1 + EU * i)
                    if c >= 2:
                        act.wait_ge(sem("e_sqsum"), c - 1 + EU * i)
                    act.activation(bsq[:, c % 2, :], bank[3][:], ACT.Square).then_inc(sem("e_bsq"), 1)
                c = k + 2
                if edge(c):
                    act.wait_ge(sem("e_ms1"), c + 1 + EU * i)
                    if c >= 2:
                        act.wait_ge(sem("e_turned_d"), c - 1 + EU * i)
                    for j in range(TILES):
                        last = act.activation(hd[:, c % 2, j, :], xd[:, c % 4, j, :], ACT.Identity,
                                              scale=rs1[:, c % 2, TILES + j:TILES + j + 1], bias=ms1[:, c % 2, j:j + 1])
                    last.then_inc(sem("e_norm1d"), 1)
                c = k - 1
                if edge(c):
                    act.wait_ge(sem("e_turned2"), c + 1 + EU * i)
                    if c >= 2:
                        act.wait_ge(sem("e_u_psum"), 2 * (c - 1) + 2 * EU * i)
                    act.activation(h2t[:, c % 2, :], bank[0][:], ACT.Relu).then_inc(sem("e_h2t"), 1)

                def hidden(m, b):
                    c = k - 1
                    act.wait_ge(sem("e_u_psum"), 2 * c + m + 1 + 2 * EU * i)
                    if c >= 2:
                        act.wait_ge(sem("e_out_psum"), c - 1 + EU * i)
                    act.activation(ut[:, c % 2, m, :], bank[b][:], ACT.Relu, bias=b1_col[:, m:m + 1]).then_inc(sem("e_ut"), 1)

                if edge(k - 1):
                    hidden(0, 7)
                c = k + 1
                if edge(c):
                    act.wait_ge(sem("e_mean_b"), c + 1 + EU * i)
                    if c >= 1:
                        act.wait_ge(sem("e_var"), c + EU * i)
                    act.activation(mean_b2[:], mean_b[:], ACT.Square).then_inc(sem("e_mean_b2"), 1)
                if edge(k - 1):
                    hidden(1, 1)
                c = k + 1
                if edge(c):
                    act.wait_ge(sem("e_var"), c + 1 + EU * i)
                    if c >= 1:
                        act.wait_ge(sem(f"e_agg{SD}"), c + EU * i)
                    act.activation(var_pos[:], var[:], ACT.Relu).then_inc(sem("e_var_pos"), 1)
                    act.wait_ge(sem("e_var_pos"), c + 1 + EU * i)
                    if c >= 2:
                        act.wait_ge(sem("e_layer0"), TILES * (c - 1) + TILES * EU * i)
                    act.activation(agg[:, c % 2, SD, :], var_pos[:], ACT.Sqrt, bias=eps_col[:]).then_inc(sem(f"e_agg{SD}"), 1)

            run_passes(act, node_step, edge_step)

        @block.vector
        def _(dve):
            chain = sem("dve_setup")
            done = [0]

            def after(ins):
                ins.then_inc(chain, 1)
                done[0] += 1
                dve.wait_ge(chain, done[0])

            dve.memset(dst_i[:], FAR)
            dve.memset(src_i[:], 0).then_inc(sem("pad_written"), 1)
            dve.memset(eps_col[:], LN_EPS).then_inc(sem("eps_ready"), 1)
            log2 = math.log(2.0)
            for s, v in enumerate((1.0, log2, 1.0 / log2)):
                last = dve.memset(lone_std[:, s, :], math.sqrt(STD_EPS) * v)
            last.then_inc(sem("lone_std_ready"), 1)
            dve.wait_ge(sem("weights_turned"), 1)
            dve.tensor_copy(w_lin_t[:], bank[0][:, 0:P])
            dve.tensor_copy(wd_t[:], bank[0][:, P:2 * P])
            dve.tensor_copy(ws_t[:], bank[0][:, 2 * P:3 * P]).then_inc(sem("weights_copied"), 1)
            dve.wait_ge(sem("weights_in"), 16 * 13)
            dve.tensor_copy(b_post_wide[:], b_post_col[:].to_broadcast([P, P])).then_inc(sem("b_post_ready"), 1)
            dve.wait_ge(sem("comb_ready"), 1)
            dve.tensor_copy(comb_x[:], bank[1][:, 0:P])
            for b in range(1, 13):
                s, a = (b - 1) // AGGS, (b - 1) % AGGS
                last = dve.tensor_copy(comb_agg[:, a, s, :], bank[1 + b // 4][:, b % 4 * P:(b % 4 + 1) * P])
            last.then_inc(sem("comb_copied"), 1)
            dve.wait_ge(sem("const_psum"), 1)
            for j in range(TILES):
                last = dve.tensor_tensor(edge_const[:, j, :], bank[5][:, 0:P], b_lin_all[:], ALU.add)
                last.then_inc(sem("const_ready"), 1)
            dve.wait_ge(sem("const_ready"), TILES)
            dve.wait_ge(sem("const_psum"), 2)
            for j in range(TILES):
                last = dve.tensor_tensor(lone_const[:, j, :], bank[6][:, 0:P], edge_const[:, j, :], ALU.add)
                last.then_inc(sem("const_ready"), 1)

            R = slice(0, ROWS)
            dve.wait_ge(sem("edge_list_in"), 16 * 5)
            dve.wait_ge(sem("pos_ready"), 1)
            dve.tensor_copy(pos1[R], pos_i[R])
            dve.tensor_copy(to_turn[R, 0, :], src_i[R]).then_inc(sem("to_turn_ready"), 1)
            after(dve.tensor_copy(dst_f[R], dst_i[R]))
            dve.tensor_scalar(to_turn[R, 1, :], dst_f[R, 1:RW + 1], float(N - 1), None, ALU.min).then_inc(sem("to_turn_ready"), 1)
            dve.tensor_tensor(first[R], dst_f[R, 1:RW + 1], dst_f[R, 0:RW], ALU.not_equal)
            after(dve.tensor_tensor(final[R], dst_f[R, 1:RW + 1], dst_f[R, 2:RW + 2], ALU.not_equal))
            dve.tensor_scalar(keep_sb[R], first[R], -1.0, 1.0, ALU.mult, ALU.add)
            dve.tensor_scalar(reset_sb[R], first[R], RESET, None, ALU.mult)
            dve.tensor_scalar(lift_sb[R], first[R], -RESET, None, ALU.mult)
            after(dve.tensor_tensor(start_mark[R], first[R], pos1[R], ALU.mult))
            dve.tensor_tensor_scan(start_scan[R], start_mark[R], start_mark[R], 0.0, ALU.max, ALU.max).then_inc(sem("start_scanned"), 1)
            after(dve.tensor_scalar(far_sb[R], pos1[R], float(FAR), None, ALU.add))
            after(dve.tensor_tensor(far_diff[R], dst_f[R, 1:RW + 1], far_sb[R], ALU.subtract))
            after(dve.tensor_tensor(far_pick[R], far_diff[R], final[R], ALU.mult))
            dve.tensor_tensor(to_turn[R, 2, :], far_pick[R], far_sb[R], ALU.add).then_inc(sem("to_turn_ready"), 1)
            dve.memset(row_carry[:], 0.0)
            dve.wait_ge(sem("row_max_psum"), 1)
            after(dve.tensor_copy(row_max[0:1, R], bank[7][0:1, 0:ROWS]))
            dve.tensor_tensor_scan(row_carry[0:1, 1:ROWS], row_max[0:1, 0:ROWS - 1], row_max[0:1, 0:ROWS - 1], 0.0,
                                   ALU.max, ALU.max).then_inc(sem("row_carry_ready"), 1)
            dve.wait_ge(sem("carry_psum"), 1)
            after(dve.tensor_copy(carry_col[R], bank[7][0:ROWS, P:P + 1]))
            after(dve.tensor_scalar(seg_start[R], start_scan[R], carry_col[R], None, ALU.max))
            dve.scalar_tensor_tensor(count[R], pos1[R], 1.0, seg_start[R], ALU.add, ALU.subtract).then_inc(sem("count_ready"), 1)
            dve.wait_ge(sem("count_ready"), 1)
            dve.reciprocal(inv_count[R], count[R]).then_inc(sem("masks_done"), 1)
            dve.wait_ge(sem("amp_ready"), 1)
            dve.reciprocal(to_turn[R, 4, :], to_turn[R, 3, :]).then_inc(sem("to_turn_ready"), 2)
            for n in range(5):
                for h in range(2):
                    dve.wait_ge(sem("turned"), 2 * n + h + 1)
                    to = index[:, n, :, h] if n < 3 else scale[:, n - 3, :, h]
                    dve.tensor_copy(to, bank[h][:, 0:ROWS]).then_inc(sem("turned_out"), 1)

            def node_step(k, i):
                if node(k + 3):
                    c, b, s = k + 3, (k + 3) % 2, (k + 3) % 4
                    dve.wait_ge(sem(f"n_in{s}"), 16 * (c // 4 + 1) + 16 * i)
                    for j in range(TILES):
                        last = dve.bn_stats(nbn1[:, b, j, :], nx[:, s, j, :])
                    last.then_inc(sem("n_bn1"), 1)
                    dve.wait_ge(sem("n_bn1"), c + 1 + NU * i)
                if node(k + 2):
                    c, b = k + 2, k % 2
                    dve.wait_ge(sem("n_sd1"), c + 1 + NU * i)
                    dve.reciprocal(nrs1[:, b, :], nsd1[:, b, :]).then_inc(sem("n_rs1"), 1)
                if node(k + 3):
                    c, b = k + 3, (k + 3) % 2
                    for j in range(TILES):
                        last = dve.bn_aggr(nmv1[:, b, j, :], nbn1[:, b, j, :])
                    last.then_inc(sem("n_mv1"), 1)
                if node(k):
                    c, b = k, k % 2
                    dve.wait_ge(sem("n_sd2"), c + 1 + NU * i)
                    if c >= 2:
                        dve.wait_ge(sem("n_norm2"), c - 1 + NU * i)
                    dve.reciprocal(nrs2[:, b, :], nsd2[:, b, :]).then_inc(sem("n_rs2"), 1)
                if node(k + 2):
                    c, b, s = k + 2, k % 2, (k + 2) % 4
                    dve.wait_ge(sem("n_rs1"), c + 1 + NU * i)
                    if c >= 2:
                        dve.wait_ge(sem("n_turn1"), c - 1 + NU * i)
                    for j in range(TILES):
                        last = dve.tensor_scalar(nh[:, b, j, :], nx[:, s, j, :], nmv1[:, b, j, 0:1], nrs1[:, b, j:j + 1],
                                                 ALU.subtract, ALU.mult)
                        if j == 0 and node(k):
                            dve.wait_ge(sem("n_rs2"), k + 1 + NU * i)
                            dve.scalar_tensor_tensor(nms2[:, b, :], nmv2[:, b, :, 0], -1.0, nrs2[:, b, :],
                                                     ALU.mult, ALU.mult).then_inc(sem("n_ms2"), 1)
                    last.then_inc(sem("n_norm1"), 1)
                elif node(k):
                    b = k % 2
                    dve.wait_ge(sem("n_rs2"), k + 1)
                    dve.scalar_tensor_tensor(nms2[:, b, :], nmv2[:, b, :, 0], -1.0, nrs2[:, b, :],
                                             ALU.mult, ALU.mult).then_inc(sem("n_ms2"), 1)
                if node(k - 2):
                    c, b = k - 2, k % 2
                    dve.wait_ge(sem("n_out_psum"), c + 1 + NU * i)
                    dve.wait_ge(sem("n_x1b"), c + 1 + NU * i)
                    if c >= 2:
                        dve.wait_ge(sem(f"n_stored{b}"), 16 * (c // 2) + 8 * NU * i)
                    dve.tensor_tensor(nout[:, b], bank[5][:].rearrange("p (j f) -> p j f", j=TILES), nx1b[:, c % 4],
                                      ALU.add).then_inc(sem("n_out"), 1)
                if node(k + 1):
                    c, b = k + 1, (k + 1) % 2
                    dve.wait_ge(sem("n_y_psum"), c + 1 + NU * i)
                    dve.wait_ge(sem("n_xc"), c + 1 + NU * i)
                    if c >= 2:
                        dve.wait_ge(sem("n_x1b"), c - 1 + NU * i)
                        dve.wait_ge(sem("n_norm2"), c - 1 + NU * i)
                    dve.tensor_tensor(nx1[:, b], bank[1][:].rearrange("p (j f) -> p j f", j=TILES), nxc[:, b],
                                      ALU.add).then_inc(sem("n_x1"), 1)
                    dve.wait_ge(sem("n_x1"), c + 1 + NU * i)
                    for j in range(TILES):
                        last = dve.bn_stats(nbn2[:, b, j, :], nx1[:, b, j, :])
                    last.then_inc(sem("n_bn2"), 1)
                    dve.wait_ge(sem("n_bn2"), c + 1 + NU * i)
                    dve.memset(stats_go[:], 0.0)
                    for j in range(TILES):
                        last = dve.bn_aggr(nmv2[:, b, j, :], nbn2[:, b, j, :])
                    last.then_inc(sem("n_mv2"), 1)

            def mix(c, j, i):
                b = c % 2
                acc = bank[5 + j % 2]
                dve.wait_ge(sem("e_layer0"), TILES * c + j + 1 + TILES * EU * i)
                if j == 0:
                    dve.wait_ge(sem("e_xdc"), c + 1 + EU * i)
                    dve.wait_ge(sem("e_scale"), c + 1 + EU * i)
                    if c >= 2:
                        dve.wait_ge(sem("e_x1b"), c - 1 + EU * i)
                        dve.wait_ge(sem("e_norm2"), c - 1 + EU * i)
                dve.scalar_tensor_tensor(part[:, j % 2, :], acc[:, P:2 * P], amp_att[:, c % 4, 0, j:j + 1], xdc[:, c % 4, j, :],
                                         ALU.mult, ALU.add).then_inc(sem("e_part"), 1)
                dve.wait_ge(sem("e_part"), TILES * c + j + 1 + TILES * EU * i)
                dve.scalar_tensor_tensor(part2[:, j % 2, :], acc[:, 2 * P:3 * P], amp_att[:, c % 4, 1, j:j + 1], part[:, j % 2, :],
                                         ALU.mult, ALU.add).then_inc(sem("e_part2"), 1)
                dve.wait_ge(sem("e_part2"), TILES * c + j + 1 + TILES * EU * i)
                ins = dve.tensor_tensor(x1[:, b, j, :], acc[:, 0:P], part2[:, j % 2, :], ALU.add)
                ins.then_inc(sem("e_mixed"), 1)

            def edge_step(k, i):
                if edge(k + 2):
                    c, b, s = k + 2, k % 2, (k + 2) % 4
                    dve.wait_ge(sem(f"e_gathered{s}"), 16 * 2 * TILES * (c // 4 + 1) + 16 * 2 * TILES * i)
                    for n, rows in ((0, xs), (1, xd)):
                        for j in range(TILES):
                            last = dve.bn_stats(bn1[:, b, n * TILES + j, :], rows[:, s, j, :])
                    last.then_inc(sem("e_bn1"), 1)
                    dve.wait_ge(sem("e_bn1"), c + 1 + EU * i)
                if edge(k - 1):
                    c, b = k - 1, (k - 1) % 2
                    dve.wait_ge(sem("e_sd2"), c + 1 + EU * i)
                    if c >= 2:
                        dve.wait_ge(sem("e_norm2"), c - 1 + EU * i)
                    dve.reciprocal(rs2[:, b, :], sd2[:, b, :]).then_inc(sem("e_rs2"), 1)
                    dve.wait_ge(sem("e_rs2"), c + 1 + EU * i)
                    dve.scalar_tensor_tensor(ms2[:, b, :], mv2[:, b, :, 0], -1.0, rs2[:, b, :],
                                             ALU.mult, ALU.mult).then_inc(sem("e_ms2"), 1)
                if edge(k + 2):
                    b = k % 2
                    for j in range(2 * TILES):
                        last = dve.bn_aggr(mv1[:, b, j, :], bn1[:, b, j, :])
                    last.then_inc(sem("e_mv1"), 1)
                c = k + 2
                if edge(c):
                    b, s = c % 2, c % 4
                    dve.wait_ge(sem("e_sd1"), c + 1 + EU * i)
                    if c >= 2:
                        dve.wait_ge(sem("e_norm1d"), c - 1 + EU * i)
                    dve.reciprocal(rs1[:, b, :], sd1[:, b, :]).then_inc(sem("e_rs1"), 1)
                    dve.wait_ge(sem("e_rs1"), c + 1 + EU * i)
                    dve.scalar_tensor_tensor(ms1[:, b, :], mv1[:, b, TILES:, 0], -1.0, rs1[:, b, TILES:],
                                             ALU.mult, ALU.mult).then_inc(sem("e_ms1"), 1)
                    if c >= 2:
                        dve.wait_ge(sem("e_turned_s"), c - 1 + EU * i)
                    for j in range(TILES):
                        last = dve.tensor_scalar(hs[:, b, j, :], xs[:, s, j, :], mv1[:, b, j, 0:1], rs1[:, b, j:j + 1],
                                                 ALU.subtract, ALU.mult)
                    last.then_inc(sem("e_norm1"), 1)
                c = k
                if edge(c):
                    b, s = c % 2, c % 4
                    dve.wait_ge(sem(f"e_masks_in{s}"), 64 * (c // 4 + 1) + 64 * i)
                    dve.wait_ge(sem("e_turned_attr"), c + 1 + EU * i)
                    if c >= 1:
                        dve.wait_ge(sem("e_attr_run"), c + EU * i)
                    if c >= 2:
                        dve.wait_ge(sem("e_attr_mean"), c - 1 + EU * i)
                    before = run_attr[:, 1 - b, CHUNK - 1:CHUNK] if c else 0.0
                    dve.tensor_tensor_scan(run_attr[:, b, :], keep[:, s, :], bank[2][:], before,
                                           ALU.mult, ALU.add).then_inc(sem("e_attr_run"), 1)
                c = k + 1
                if edge(c):
                    b, s = c % 2, c % 4
                    dve.wait_ge(sem("e_bsq"), c + 1 + EU * i)
                    dve.wait_ge(sem(f"e_masks_in{s}"), 64 * (c // 4 + 1) + 64 * i)
                    if c:
                        dve.wait_ge(sem("e_sqsum"), c + EU * i)
                    end = slice(CHUNK - 1, CHUNK)
                    dve.tensor_tensor_scan(run_max[:, b, :], reset[:, s, :], bank[3][:],
                                           run_max[:, 1 - b, end] if c else 0.0, ALU.add, ALU.max).then_inc(sem("e_max"), 1)
                    dve.tensor_tensor_scan(run_min[:, b, :], lift[:, s, :], bank[3][:],
                                           run_min[:, 1 - b, end] if c else 0.0, ALU.add, ALU.min).then_inc(sem("e_min"), 1)
                if edge(k):
                    mix(k, 0, i)
                if edge(c):
                    dve.tensor_tensor_scan(run_sum[:, b, :], keep[:, s, :], bank[3][:],
                                           run_sum[:, 1 - b, end] if c else 0.0, ALU.mult, ALU.add).then_inc(sem("e_sum"), 1)
                    dve.tensor_tensor_scan(run_sq[:, b, :], keep[:, s, :], bsq[:, b, :],
                                           run_sq[:, 1 - b, end] if c else 0.0, ALU.mult, ALU.add).then_inc(sem("e_sqsum"), 1)
                if edge(k):
                    mix(k, 1, i)
                if edge(c):
                    dve.wait_ge(sem("e_a_psum"), c + 1 + EU * i)
                    dve.wait_ge(sem("e_sum"), c + 1 + EU * i)
                    dve.wait_ge(sem("e_max"), c + 1 + EU * i)
                    dve.wait_ge(sem("e_min"), c + 1 + EU * i)
                    if c >= 2:
                        dve.wait_ge(sem("e_layer0"), TILES * (c - 1) + TILES * EU * i)
                    if c >= 1:
                        dve.wait_ge(sem("e_mean_b2"), c + EU * i)
                    dve.tensor_tensor(mean_b[:], run_sum[:, b, :], inv[:, s, :], ALU.mult).then_inc(sem("e_mean_b"), 1)
                    dve.scalar_tensor_tensor(agg[:, b, MX, :], bank[4][:], b_pre_col[:], run_max[:, b, :],
                                             ALU.add, ALU.add).then_inc(sem(f"e_agg{MX}"), 1)
                    dve.scalar_tensor_tensor(agg[:, b, MN, :], bank[4][:], b_pre_col[:], run_min[:, b, :],
                                             ALU.add, ALU.add).then_inc(sem(f"e_agg{MN}"), 1)
                if edge(k):
                    mix(k, 2, i)
                if edge(c):
                    dve.wait_ge(sem("e_sqsum"), c + 1 + EU * i)
                    dve.tensor_tensor(sq_mean[:], run_sq[:, b, :], inv[:, s, :], ALU.mult).then_inc(sem("e_sq_mean"), 1)
                    dve.wait_ge(sem("e_mean_b"), c + 1 + EU * i)
                    dve.scalar_tensor_tensor(agg[:, b, ME, :], bank[4][:], b_pre_col[:], mean_b[:],
                                             ALU.add, ALU.add).then_inc(sem(f"e_agg{ME}"), 1)
                    dve.wait_ge(sem("e_sq_mean"), c + 1 + EU * i)
                    dve.wait_ge(sem("e_mean_b2"), c + 1 + EU * i)
                    if c >= 1:
                        dve.wait_ge(sem("e_var_pos"), c + EU * i)
                    dve.tensor_tensor(var[:], sq_mean[:], mean_b2[:], ALU.subtract).then_inc(sem("e_var"), 1)
                    dve.wait_ge(sem("e_var"), c + 1 + EU * i)
                    dve.wait_ge(sem(f"e_agg{ME}"), c + 1 + EU * i)
                if edge(k):
                    c, b = k, k % 2
                    mix(c, 3, i)
                    dve.wait_ge(sem("e_mixed"), TILES * (c + 1) + TILES * EU * i)
                    for j in range(TILES):
                        last = dve.bn_stats(bn2[:, b, j, :], x1[:, b, j, :])
                    last.then_inc(sem("e_bn2"), 1)
                    dve.wait_ge(sem("e_bn2"), c + 1 + EU * i)
                if edge(k - 1):
                    c, b = k - 1, (k - 1) % 2
                    dve.wait_ge(sem("e_out_psum"), c + 1 + EU * i)
                    dve.wait_ge(sem("e_x1b"), c + 1 + EU * i)
                    if c == 0:
                        for n in range(2):
                            dve.wait_ge(sem(f"n_stored{n}"), 16 * ((NODE_CHUNKS - n + 1) // 2))
                    if c >= 2:
                        dve.wait_ge(sem(f"e_scattered{(c - 2) % 4}"), 16 * TILES * ((c - 2) // 4 + 1) + 16 * TILES * i)
                    dve.tensor_tensor(eout[:, b], bank[7][:].rearrange("p (j f) -> p j f", j=TILES), x1b[:, c % 4],
                                      ALU.add).then_inc(sem("e_out"), 1)
                if edge(k):
                    b = k % 2
                    for j in range(TILES):
                        last = dve.bn_aggr(mv2[:, b, j, :], bn2[:, b, j, :])
                    last.then_inc(sem("e_mv2"), 1)

            run_passes(dve, node_step, edge_step)


_NAMES = ["x", "src", "dst", "edge_attr_128", "L0_gnn_W_pre", "L0_gnn_b_pre", "L0_gnn_W_post", "L0_gnn_b_post",
          "L0_gnn_W_lin", "L0_gnn_b_lin", "L1_gnn_W1", "L1_gnn_b1", "L1_gnn_W2", "L1_gnn_b2"]


def kernel(**inputs):
    import numpy as np
    import concourse.bacc as bacc
    from concourse.bass_utils import run_bass_kernel_spmd

    nc = bacc.Bacc("TRN2", target_bir_lowering=False, num_devices=1)
    arrays, args = {}, []
    for name in _NAMES:
        a = np.ascontiguousarray(inputs[name])
        arrays[f"in_{name}"] = a
        args.append(nc.dram_tensor(f"in_{name}", a.shape, mybir.dt.from_np(a.dtype), kind="ExternalInput").ap())
    y = nc.dram_tensor("y", arrays["in_x"].shape, mybir.dt.float32, kind="ExternalOutput").ap()
    build(nc, *args, y)
    r = run_bass_kernel_spmd(nc, [arrays], core_ids=[0])
    return r.results[0]["y"]
```

```python
import math

import concourse.bass as bass
from concourse import mybir

ALU = mybir.AluOpType
ACT = mybir.ActivationFunctionType
F32 = mybir.dt.float32
BF16 = mybir.dt.bfloat16
F32R = mybir.dt.float32r
I32 = mybir.dt.int32

P = 128
TILES = 4
CHUNK = P * TILES
LN_EPS = 1e-5
STD_EPS = 1e-5
FAR = 1 << 20
RESET = -3.0e38
AGGS = 4
SCALERS = 3
MX, MN, ME, SD = range(AGGS)


def build(nc, x, src, dst, edge_attr, w_pre, b_pre, w_post, b_post, w_lin, b_lin, w1, b1, w2, b2, out):
    N, F = x.shape
    E = src.shape[0]
    HID = w1.shape[1]
    assert F == P and HID == 2 * P and N >= CHUNK and N < FAR
    NODE_CHUNKS = -(-N // CHUNK)
    EDGE_CHUNKS = -(-E // CHUNK)
    ROWS = 2 * EDGE_CHUNKS
    RW = 2 * P
    FULL_ROWS = E // RW
    REST = E - FULL_ROWS * RW
    assert ROWS <= P and FULL_ROWS == ROWS - 1 and REST > 0
    LAST_EDGE_ROWS = E - (EDGE_CHUNKS - 1) * CHUNK

    keep_row = nc.dram_tensor("keep_row", [ROWS * RW], BF16, kind="Internal").ap()
    reset_row = nc.dram_tensor("reset_row", [ROWS * RW], BF16, kind="Internal").ap()
    lift_row = nc.dram_tensor("lift_row", [ROWS * RW], BF16, kind="Internal").ap()
    inv_row = nc.dram_tensor("inv_row", [ROWS * RW], F32, kind="Internal").ap()

    def sb(name, shape, dt=F32):
        return nc.alloc_sbuf_tensor(name, shape, dt)

    bank = [nc.alloc_psum_tensor(f"bank{i}", [P, CHUNK], F32) for i in range(8)]
    sems = {}

    def sem(name):
        if name not in sems:
            sems[name] = nc.alloc_semaphore(name)
        return sems[name]

    ident = sb("ident", [P, P])
    w_pre_sb = sb("w_pre_sb", [P, 2 * P])
    attr = sb("attr", [P, 2, TILES, P])
    w_lin_sb = sb("w_lin_sb", [P, P])
    w_lin_t = sb("w_lin_t", [P, P])
    wd_t = sb("wd_t", [P, P])
    wd_hi = sb("wd_hi", [P, P], F32R)
    wd_lo = sb("wd_lo", [P, P], F32R)
    comb_x_hi = sb("comb_x_hi", [P, P], F32R)
    comb_x_lo = sb("comb_x_lo", [P, P], F32R)
    ws_t = sb("ws_t", [P, P])
    comb_x = sb("comb_x", [P, P])
    comb_hi = sb("comb_hi", [P, AGGS - 1, SCALERS, P], F32R)
    comb_lo = sb("comb_lo", [P, AGGS - 1, SCALERS, P], F32R)
    comb_sd = sb("comb_sd", [P, SCALERS, P])
    w1_hi = sb("w1_hi", [P, 2, HID], F32R)
    w1_lo = sb("w1_lo", [P, 2, HID], F32R)
    w2_sb = sb("w2_sb", [P, 2, P])
    w1_attr = sb("w1_attr", [P, HID])
    b1_col = sb("b1_col", [P, 2])
    b_pre_col = sb("b_pre_col", [P, 1])
    b_post_col = sb("b_post_col", [P, 1])
    b_post_wide = sb("b_post_wide", [P, P])
    b_lin_all = sb("b_lin_all", [P, P])
    b2_all = sb("b2_all", [P, TILES, P])
    edge_const = sb("edge_const", [P, TILES, P])
    lone_const = sb("lone_const", [P, TILES, P])
    lone_std = sb("lone_std", [P, SCALERS, P])
    eps_col = sb("eps_col", [P, 1])
    PAIR, LOW = 64, 32
    ones = sb("ones", [PAIR, P], F32R)
    b2_hi = sb("b2_hi", [PAIR, CHUNK], F32R)
    b2_rows = sb("b2_rows", [PAIR, CHUNK], F32R)

    hd = sb("hd", [P, 2, TILES, P])
    hd_flat = hd[:].rearrange("p b j f -> p (b j f)")
    dst_i = hd_flat[:, 0:RW + 2].bitcast(I32)
    dst_f = hd_flat[:, RW + 2:2 * RW + 4]
    src_i = hd_flat[:, 2 * RW + 4:3 * RW + 4].bitcast(I32)
    runs = sb("runs", [P, 5, 2, CHUNK])
    work = runs[:, 0:4].rearrange("p q b (n w) -> p (q b n) w", w=RW)
    pos_i = work[:, 15, :].bitcast(I32)
    first = work[:, 0, :]
    final = work[:, 1, :]
    pos1 = work[:, 2, :]
    start_mark = work[:, 3, :]
    start_scan = work[:, 4, :]
    seg_start = work[:, 5, :]
    row_max = sb("row_max", [1, P])
    row_carry = sb("row_carry", [1, P])
    carry_col = sb("carry_col", [P, 1])
    count = work[:, 6, :]
    inv_count = sb("inv_count", [P, RW])
    keep_sb = sb("keep_sb", [P, RW], BF16)
    reset_sb = sb("reset_sb", [P, RW], BF16)
    lift_sb = sb("lift_sb", [P, RW], BF16)
    far_sb = work[:, 7, :]
    far_diff = work[:, 8, :]
    far_pick = work[:, 9, :]
    to_turn = work[:, 10:15, :]
    index = sb("index", [P, 3, ROWS, 2], I32)
    scale = sb("scale", [P, 2, ROWS, 2])

    nx1 = sb("nx1", [P, 2, TILES, P])
    nx1b = runs[:, 0:2].rearrange("p q b (j f) -> p (q b) j f", f=P)
    nh2 = sb("nh2", [P, 2, TILES, P])
    nh2t = sb("nh2t", [P, 2, CHUNK], F32R)
    nut = sb("nut", [P, 2, 2, CHUNK])
    nh2l = sb("nh2l", [P, 2, CHUNK], F32R)
    nout = sb("nout", [P, 2, TILES, P])
    nbn1 = sb("nbn1", [P, 2, TILES, 6])
    nmv1 = sb("nmv1", [P, 4, TILES, 2])
    nsd1 = sb("nsd1", [P, 2, TILES])
    nrs1 = sb("nrs1", [P, 4, TILES])
    nms1 = sb("nms1", [P, 4, 1])
    nbn2 = sb("nbn2", [P, 2, TILES, 6])
    nmv2 = sb("nmv2", [P, 2, TILES, 2])
    nsd2 = sb("nsd2", [P, 2, TILES])
    nrs2 = sb("nrs2", [P, 2, TILES])
    nms2 = sb("nms2", [P, 2, TILES])

    xs = sb("xs", [P, 4, TILES, P])
    nx = xs
    xd = sb("xd", [P, 4, TILES, P])
    w_post_sb = xd[:].rearrange("p s j f -> p (s j f)")[:, 0:13 * P]
    xdc = sb("xdc", [P, 2, TILES, P])
    nxc = xdc
    keep = sb("keep", [P, 4, CHUNK], BF16)
    reset = sb("reset", [P, 4, CHUNK], BF16)
    lift = sb("lift", [P, 4, CHUNK], BF16)
    inv = sb("inv", [P, 4, CHUNK])
    idx = sb("idx", [P, 4, 2, TILES], I32)
    stats_go = sb("stats_go", [P, 1])
    gather_go = sb("gather_go", [P, 1])
    oidx = sb("oidx", [P, 4, TILES], I32)
    amp_att = sb("amp_att", [P, 4, 2, TILES])
    bn1 = sb("bn1", [P, 2, 2 * TILES, 6])
    mv1 = sb("mv1", [P, 2, 2 * TILES, 2])
    sd1 = sb("sd1", [P, 2, 2 * TILES])
    rs1 = sb("rs1", [P, 2, 2 * TILES])
    ms1 = sb("ms1", [P, 2, 2 * TILES])
    hs = sb("hs", [P, 2, TILES, P])
    nh = hs
    hst = sb("hst", [P, 2, CHUNK])
    nht = hst
    hdt = sb("hdt", [P, 2, CHUNK], F32R)
    hdl = sb("hdl", [P, 2, CHUNK], F32R)
    bsq = sb("bsq", [P, 2, CHUNK])
    run_max, run_min, run_sum, run_sq, run_attr = (runs[:, q] for q in range(5))
    w1_sb = run_attr.rearrange("p b (k h) -> p (b k) h", h=HID)[:, 0:2, :]
    mean_b = sb("mean_b", [P, CHUNK])
    mean_b2 = sb("mean_b2", [P, CHUNK])
    var = sb("var", [P, CHUNK])
    whole = sb("whole", [P, 2, CHUNK])
    agg_hi = sb("agg_hi", [P, 2, AGGS - 1, CHUNK], F32R)
    agg_lo = sb("agg_lo", [P, 2, AGGS - 1, CHUNK], F32R)
    agg_sd = sb("agg_sd", [P, 2, CHUNK])
    attr_mean = sb("attr_mean", [P, 2, CHUNK])
    part = sb("part", [P, 2, P])
    part2 = sb("part2", [P, 2, P])
    x1 = nx1
    bn2 = sb("bn2", [P, 2, TILES, 6])
    mv2 = sb("mv2", [P, 2, TILES, 2])
    sd2 = sb("sd2", [P, 2, TILES])
    rs2 = sb("rs2", [P, 2, TILES])
    ms2 = sb("ms2", [P, 2, TILES])
    h2 = nh2
    h2t = nh2t
    h2l = nh2l
    ut = nut
    eout = nout

    NU, EU = 4, 4
    N_LO, N_HI, N_LOOP = -6, NODE_CHUNKS + 3, 6
    N_LOOPS = (NODE_CHUNKS - 7 - N_LOOP) // NU
    E_LO, E_HI, E_LOOP = -4, EDGE_CHUNKS + 2, 4
    E_LOOPS = (EDGE_CHUNKS - 5 - E_LOOP) // EU

    def run_passes(eng, node_step, edge_step):
        for k in range(N_LO, N_LOOP):
            node_step(k, 0)
        with eng.Fori(0, N_LOOPS) as i:
            for u in range(NU):
                node_step(N_LOOP + u, i)
        for k in range(N_LOOP + N_LOOPS * NU, N_HI):
            node_step(k, 0)
            if k - N_HI >= E_LO:
                edge_step(k - N_HI, 0)
        for k in range(0, E_LOOP):
            edge_step(k, 0)
        with eng.Fori(0, E_LOOPS) as i:
            for u in range(EU):
                edge_step(E_LOOP + u, i)
        for k in range(E_LOOP + E_LOOPS * EU, E_HI):
            edge_step(k, 0)

    def node(c):
        return 0 <= c < NODE_CHUNKS

    def edge(c):
        return 0 <= c < EDGE_CHUNKS

    def node_rows(ap, c, i):
        base = min(c * CHUNK, N - CHUNK) + i * (NU * CHUNK)
        return ap[bass.ds(base, CHUNK), :].rearrange("(p j) f -> p j f", j=TILES)

    with nc.Block() as block:

        @block.sync
        def _(sp):
            w = sem("weights_in")
            sp.dma_start(w_lin_sb[:], w_lin).then_inc(w, 16)
            sp.dma_start(w_pre_sb[:], w_pre).then_inc(w, 16)
            sp.dma_start(w_post_sb, w_post).then_inc(w, 16)
            sp.dma_start(w1_sb, w1.rearrange("(k p) h -> p k h", p=P)).then_inc(w, 16)
            sp.dma_start(w2_sb[:], w2.rearrange("(k p) h -> p k h", p=P)).then_inc(w, 16)
            sp.dma_start(b_lin_all[:], b_lin.rearrange("(a f) -> a f", a=1).to_broadcast([P, P])).then_inc(w, 16)
            for j in range(TILES):
                sp.dma_start(b2_all[:, j, :], b2.rearrange("(a f) -> a f", a=1).to_broadcast([P, P])).then_inc(w, 16)
            with nc.allow_non_contiguous_dma(reason="a bias as one value per partition"):
                sp.dma_start(b1_col[:], b1.rearrange("(k p) -> p k", p=P)).then_inc(w, 16)
                sp.dma_start(b_pre_col[:], b_pre.rearrange("(p a) -> p a", a=1)).then_inc(w, 16)
                sp.dma_start(b_post_col[:], b_post.rearrange("(p a) -> p a", a=1)).then_inc(w, 16)

            sp.wait_ge(sem("pad_written"), 1)
            e = sem("edge_list_in")
            d = dst.tensor
            sp.dma_start(dst_i[0:1, 1:RW + 2], bass.AP(tensor=d, offset=0, ap=[[RW + 1, 1], [1, RW + 1]])).then_inc(e, 16)
            sp.dma_start(dst_i[1:FULL_ROWS, :],
                         bass.AP(tensor=d, offset=RW - 1, ap=[[RW, FULL_ROWS - 1], [1, RW + 2]])).then_inc(e, 16)
            sp.dma_start(dst_i[FULL_ROWS:ROWS, 0:REST + 1],
                         bass.AP(tensor=d, offset=FULL_ROWS * RW - 1, ap=[[REST + 1, 1], [1, REST + 1]])).then_inc(e, 16)
            sp.dma_start(src_i[0:FULL_ROWS, :], src[0:FULL_ROWS * RW].rearrange("(r w) -> r w", w=RW)).then_inc(e, 16)
            sp.dma_start(src_i[FULL_ROWS:ROWS, 0:REST],
                         src[FULL_ROWS * RW:E].rearrange("(a w) -> a w", a=1)).then_inc(e, 16)

            sp.wait_ge(sem("masks_done"), 1)
            r = sem("rows_out")
            sp.dma_start(keep_row.rearrange("(r w) -> r w", w=RW), keep_sb[0:ROWS, :]).then_inc(r, 16)
            sp.dma_start(reset_row.rearrange("(r w) -> r w", w=RW), reset_sb[0:ROWS, :]).then_inc(r, 16)
            sp.dma_start(lift_row.rearrange("(r w) -> r w", w=RW), lift_sb[0:ROWS, :]).then_inc(r, 16)
            sp.dma_start(inv_row.rearrange("(r w) -> r w", w=RW), inv_count[0:ROWS, :]).then_inc(r, 16)

            def node_step(k, i):
                c = k + 6
                if node(c):
                    if c >= 4:
                        sp.wait_ge(sem("n_norm1"), c - 3 + NU * i)
                        sp.wait_ge(sem("n_norm1_act"), c - 3 + NU * i)
                        sp.wait_ge(sem("n_norm1_pool"), c - 3 + NU * i)
                        sp.wait_ge(sem("n_xc"), c - 3 + NU * i)
                    sp.dma_start(nx[:, c % 4], node_rows(x, c, i)).then_inc(sem(f"n_in{c % 4}"), 16)
                c = k - 3
                if node(c):
                    sp.wait_ge(sem("n_out"), c + 1 + NU * i)
                    if c == NODE_CHUNKS - 1:
                        sp.wait_ge(sem(f"n_stored{(c - 1) % 2}"), 16 * ((c - 1) // 2 + 1))
                    sp.dma_start(node_rows(out, c, i), nout[:, c % 2]).then_inc(sem(f"n_stored{c % 2}"), 16)

            def edge_step(k, i):
                c = k + 4
                if edge(c):
                    s = c % 4
                    if c == 0:
                        sp.wait_ge(r, 64)
                    if c >= 4:
                        sp.wait_ge(sem("e_attr_mean"), c - 3 + EU * i)
                    m = sem(f"e_masks_in{s}")
                    for dst_sb, row in ((keep, keep_row), (reset, reset_row), (lift, lift_row), (inv, inv_row)):
                        sp.dma_start(dst_sb[:, s, :],
                                     row[bass.ds(c * CHUNK + i * (EU * CHUNK), CHUNK)]
                                     .rearrange("(a w) -> a w", a=1).to_broadcast([P, CHUNK])).then_inc(m, 16)
                c = k + 2
                if edge(c):
                    s = c % 2
                    if c >= 2:
                        sp.wait_ge(sem("e_turned_attr"), c - 1 + EU * i)
                    a = sem(f"e_attr_in{s}")
                    if c < EDGE_CHUNKS - 1:
                        rows = edge_attr[bass.ds(c * CHUNK + i * (EU * CHUNK), CHUNK), :]
                        sp.dma_start(attr[:, s], rows.rearrange("(j p) f -> p j f", p=P)).then_inc(a, 16)
                    else:
                        full = LAST_EDGE_ROWS // P
                        base = c * CHUNK
                        sp.dma_start(attr[:, s, 0:full, :],
                                     edge_attr[base:base + full * P, :].rearrange("(j p) f -> p j f", p=P)).then_inc(a, 16)
                        sp.dma_start(attr[0:LAST_EDGE_ROWS - full * P, s, full, :],
                                     edge_attr[base + full * P:E, :]).then_inc(a, 16)

            run_passes(sp, node_step, edge_step)

        @block.gpsimd
        def _(pool):
            fixed = sem("ident_ready")
            pool.memset(ident[:], 0.0).then_inc(sem("ident_zero"), 1)
            pool.iota(pos_i, pattern=[[1, RW]], base=1, channel_multiplier=RW).then_inc(sem("pos_ready"), 1)
            pool.wait_ge(sem("ident_zero"), 1)
            pool.affine_select(out=ident[:], in_=ident[:], compare_op=ALU.not_equal, fill=1.0, base=0,
                               pattern=[[-1, P]], channel_multiplier=1).then_inc(sem("ident_ready"), 1)
            pool.wait_ge(sem("const_ready"), 2 * TILES)

            def node_step(k, i):
                c = k
                if node(c):
                    pool.wait_ge(sem("n_x1"), c + 1 + NU * i)
                    if c >= 4:
                        pool.wait_ge(sem("n_out"), c - 3 + NU * i)
                    if c == 0:
                        pool.wait_ge(sem("weights_in"), 16 * 13)
                    pool.tensor_tensor(nx1b[:, c % 4], nx1[:, c % 2], b2_all[:], ALU.add).then_inc(sem("n_x1b"), 1)
                c = k + 2
                if node(c):
                    pool.wait_ge(sem(f"n_in{c % 4}"), 16 * (c // 4 + 1) + 16 * i)
                    if c >= 2:
                        pool.wait_ge(sem("n_x1"), c - 1 + NU * i)
                    pool.wait_ge(sem("n_rs1"), c + 1 + NU * i)
                    if c >= 2:
                        pool.wait_ge(sem("n_turn1"), c - 1 + NU * i)
                    pool.tensor_tensor(nxc[:, c % 2], nx[:, c % 4], lone_const[:], ALU.add).then_inc(sem("n_xc"), 1)
                    for j in (2, 3):
                        last = pool.tensor_scalar(nh[:, c % 2, j, :], nx[:, c % 4, j, :], nmv1[:, c % 4, j, 0:1],
                                                  nrs1[:, c % 4, j:j + 1], ALU.subtract, ALU.mult)
                    last.then_inc(sem("n_norm1_pool"), 1)

            def low_part(a, c, i):
                pool.wait_ge(sem(f"e_hi{a}"), c + 1 + EU * i)
                if c >= 2:
                    pool.wait_ge(sem("e_layer0"), TILES * (c - 1) + TILES * EU * i)
                pool.tensor_tensor(agg_lo[:, c % 2, a, :], whole[:, a, :], agg_hi[:, c % 2, a, :],
                                   ALU.subtract).then_inc(sem(f"e_lo{a}"), 1)

            def edge_step(k, i):
                c = k + 1
                if edge(c):
                    pool.wait_ge(sem(f"e_gathered{c % 4}"), 16 * 2 * TILES * (c // 4 + 1) + 16 * 2 * TILES * i)
                    if c == 0:
                        pool.wait_ge(sem("n_x1"), NODE_CHUNKS)
                    if c >= 2:
                        pool.wait_ge(sem("e_mixed"), TILES * (c - 1) + TILES * EU * i)
                    pool.tensor_tensor(xdc[:, c % 2], xd[:, c % 4], edge_const[:], ALU.add).then_inc(sem("e_xdc"), 1)
                    t = bass.ds(2 * c + (2 * EU) * i, 2)
                    pool.tensor_copy(amp_att[:, c % 4].rearrange("p w (r h) -> p w r h", h=2), scale[:, :, t, :]).then_inc(sem("e_scale"), 1)
                c = k - 2
                if edge(c):
                    pool.wait_ge(fixed, 1)
                    pool.wait_ge(sem("e_out"), c + 1 + EU * i)
                    if c == 0:
                        for n in range(2):
                            pool.wait_ge(sem(f"n_stored{n}"), 16 * ((NODE_CHUNKS - n + 1) // 2))
                    if c >= 4:
                        pool.wait_ge(sem(f"e_scattered{c % 4}"), 16 * TILES * (c // 4) + 16 * TILES * i)
                    t = bass.ds(2 * c + (2 * EU) * i, 2)
                    pool.tensor_copy(oidx[:, c % 4].rearrange("p (r h) -> p r h", h=2), index[:, 2, t, :]).then_inc(sem("e_oidx"), 1)
                c = k + 4
                if edge(c):
                    s = c % 4
                    pool.wait_ge(fixed, 1)
                    if c == 0:
                        pool.wait_ge(sem("turned_out"), 10)
                        pool.wait_ge(sem("n_norm1"), NODE_CHUNKS)
                        pool.wait_ge(sem("n_norm1_act"), NODE_CHUNKS)
                        pool.wait_ge(sem("n_xc"), NODE_CHUNKS)
                    if c >= 4:
                        pool.wait_ge(sem(f"e_gathered{s}"), 16 * 2 * TILES * (c // 4) + 16 * 2 * TILES * i)
                        pool.wait_ge(sem("e_norm1"), c - 3 + EU * i)
                        pool.wait_ge(sem("e_norm1d"), c - 3 + EU * i)
                        pool.wait_ge(sem("e_xdc"), c - 3 + EU * i)
                    t = bass.ds(2 * c + (2 * EU) * i, 2)
                    pool.tensor_copy(idx[:, s].rearrange("p w (r h) -> p w r h", h=2), index[:, 0:2, t, :]).then_inc(sem("e_idx"), 1)
                    pool.wait_ge(sem("e_idx"), c + 1 + EU * i)
                    if edge(k - 2):
                        pool.wait_ge(sem("e_oidx"), k - 1 + EU * i)
                    pool.tensor_tensor(gather_go[:], eps_col[:], eps_col[:], ALU.add)
                    g = sem(f"e_gathered{s}")
                    for j in range(TILES):
                        for which, rows in ((0, xs), (1, xd)):
                            pool.indirect_dma_start(
                                out=rows[:, s, j, :], out_offset=None, in_=x,
                                in_offset=bass.IndirectOffsetOnAxis(ap=idx[:, s, which, j:j + 1], axis=0)).then_inc(g, 16)
                c = k + 1
                if edge(c):
                    low_part(MX, c, i)
                    low_part(MN, c, i)
                c = k - 2
                if edge(c):
                    if not edge(k + 4):
                        pool.wait_ge(sem("e_oidx"), k - 1)
                    for j in range(TILES):
                        pool.indirect_dma_start(
                            out=out, out_offset=bass.IndirectOffsetOnAxis(ap=oidx[:, c % 4, j:j + 1], axis=0),
                            in_=eout[:, c % 2, j, :], in_offset=None,
                            bounds_check=N - 1, oob_is_err=False).then_inc(sem(f"e_scattered{c % 4}"), 16)
                c = k
                if edge(c):
                    pool.wait_ge(sem("e_attr_run"), c + 1 + EU * i)
                    if c >= 2:
                        pool.wait_ge(sem("e_u_psum"), 2 * (c - 1) + 2 * EU * i)
                    if c < 4:
                        pool.wait_ge(sem(f"e_masks_in{c % 4}"), 64)
                    pool.tensor_tensor(attr_mean[:, c % 2, :], run_attr[:, c % 2, :], inv[:, c % 4, :],
                                       ALU.mult).then_inc(sem("e_attr_mean"), 1)

            run_passes(pool, node_step, edge_step)
            for s in range(4):
                pool.wait_ge(sem(f"e_scattered{s}"), 16 * TILES * ((EDGE_CHUNKS - s + 3) // 4))

        @block.tensor
        def _(pe):
            pe.wait_ge(sem("ident_ready"), 1)
            pe.wait_ge(sem("weights_in"), 16 * 13)
            pe.transpose(bank[0][:, 0:P], w_lin_sb[:], ident[:])
            pe.transpose(bank[0][:, P:2 * P], w_pre_sb[:, 0:P], ident[:])
            pe.transpose(bank[0][:, 2 * P:3 * P], w_pre_sb[:, P:2 * P], ident[:]).then_inc(sem("weights_turned"), 1)
            pe.wait_ge(sem("weights_copied"), 1)
            for b in range(13):
                mm = pe.matmul(bank[1 + b // 4][:, b % 4 * P:(b % 4 + 1) * P], w_post_sb[:, b * P:(b + 1) * P], w_lin_t[:],
                               start=True, stop=True)
            mm.then_inc(sem("comb_ready"), 1)
            pe.wait_ge(sem("b_post_ready"), 1)
            pe.matmul(bank[5][:, 0:P], b_post_wide[:], w_lin_t[:], start=True, stop=True).then_inc(sem("const_psum"), 1)
            pe.wait_ge(sem("comb_copied"), 1)
            pe.wait_ge(sem("lone_std_ready"), 1)
            for s in range(SCALERS):
                mm = pe.matmul(bank[6][:, 0:P], lone_std[:, s, :], comb_sd[:, s, :], start=(s == 0), stop=(s == SCALERS - 1))
            mm.then_inc(sem("const_psum"), 1)
            pe.wait_ge(sem("start_scanned"), 1)
            pe.transpose(bank[7][0:1, 0:ROWS], start_scan[0:ROWS, RW - 1:RW], ident[0:ROWS, 0:ROWS]).then_inc(sem("row_max_psum"), 1)
            pe.wait_ge(sem("row_carry_ready"), 1)
            pe.transpose(bank[7][0:ROWS, P:P + 1], row_carry[0:1, 0:ROWS], ident[0:1, 0:1]).then_inc(sem("carry_psum"), 1)
            for n in range(5):
                pe.wait_ge(sem("to_turn_ready"), n + 1)
                for h in range(2):
                    if 2 * n + h >= 2:
                        pe.wait_ge(sem("turned_out"), 2 * n + h - 1)
                    pe.transpose(bank[h][:, 0:ROWS], to_turn[0:ROWS, n, h * P:(h + 1) * P],
                                 ident[0:ROWS, 0:ROWS]).then_inc(sem("turned"), 1)
            pe.wait_ge(sem("turned_out"), 10)

            def node_step(k, i):
                c = k + 1
                if node(c):
                    pe.wait_ge(sem("n_norm1"), c + 1 + NU * i)
                    pe.wait_ge(sem("n_norm1_act"), c + 1 + NU * i)
                    pe.wait_ge(sem("n_norm1_pool"), c + 1 + NU * i)
                    if c >= 1:
                        pe.wait_ge(sem("n_ht"), c + NU * i)
                    for j in range(TILES):
                        mm = pe.transpose(bank[0][:, j * P:(j + 1) * P], nh[:, c % 2, j, :], ident[:])
                    mm.then_inc(sem("n_turn1"), 1)
                c = k - 1
                if node(c):
                    pe.wait_ge(sem("n_norm2"), c + 1 + NU * i)
                    if c >= 1:
                        pe.wait_ge(sem("n_h2l"), c + NU * i)
                    for j in range(TILES):
                        mm = pe.transpose(bank[2][:, j * P:(j + 1) * P], nh2[:, c % 2, j, :], ident[:])
                    mm.then_inc(sem("n_turn2"), 1)
                c = k - 3
                if node(c):
                    pe.wait_ge(sem("n_ut"), 2 * (c + 1) + 2 * NU * i)
                    if c >= 1:
                        pe.wait_ge(sem("n_out"), c + NU * i)
                    for j in range(TILES):
                        for m in range(2):
                            mm = pe.matmul(bank[5][:, j * P:(j + 1) * P], nut[:, c % 2, m, j * P:(j + 1) * P], w2_sb[:, m, :],
                                           start=(m == 0), stop=(m == 1))
                    mm.then_inc(sem("n_out_psum"), 1)
                c = k + 1
                if node(c):
                    pe.wait_ge(sem("n_ht"), c + 1 + NU * i)
                    if c >= 1:
                        pe.wait_ge(sem("n_x1"), c + NU * i)
                    for j in range(TILES):
                        mm = pe.matmul(bank[1][:, j * P:(j + 1) * P], nht[:, c % 2, j * P:(j + 1) * P], comb_x[:],
                                       start=True, stop=True)
                    mm.then_inc(sem("n_y_psum"), 1)
                c = k - 2
                if node(c):
                    pe.wait_ge(sem("n_h2l"), c + 1 + NU * i)
                    for m in range(2):
                        if c >= 1:
                            pe.wait_ge(sem("n_ut"), 2 * c - 1 + m + 2 * NU * i)
                        cols = slice(m * P, (m + 1) * P)
                        pe.matmul(bank[6 + m][:], w1_lo[:, 0, cols], nh2t[:, c % 2, :], start=True, stop=False)
                        pe.matmul(bank[6 + m][:], w1_hi[:, 0, cols], nh2t[:, c % 2, :], start=False, stop=False)
                        pe.matmul(bank[6 + m][:], w1_hi[:, 0, cols], nh2l[:, c % 2, :], start=False, stop=True).then_inc(sem("n_u_psum"), 1)

            def layer0(c, j, i):
                acc = bank[5 + j % 2]
                if c == 0 and j == 0:
                    pe.wait_ge(sem("n_out"), NODE_CHUNKS)
                if c == 0 and j == 1:
                    pe.wait_ge(sem("n_ut"), 2 * NODE_CHUNKS)
                if j >= 2:
                    pe.wait_ge(sem("e_mixed"), TILES * c + j - 1 + TILES * EU * i)
                elif c >= 1:
                    pe.wait_ge(sem("e_mixed"), TILES * (c - 1) + j + 3 + TILES * EU * i)
                cols = slice(j * P, (j + 1) * P)
                for a in (MX, MN, ME):
                    hi, lo = agg_hi[:, c % 2, a, cols], agg_lo[:, c % 2, a, cols]
                    w_hi, w_lo = (w[:, a].rearrange("p s f -> p (s f)") for w in (comb_hi, comb_lo))
                    if j == 0:
                        pe.wait_ge(sem(f"e_hi{a}"), c + 1 + EU * i)
                    pe.matmul(acc[:, 0:SCALERS * P], hi, w_lo, start=(a == MX), stop=False, skip_group_check=True)
                    pe.matmul(acc[:, 0:SCALERS * P], hi, w_hi, start=False, stop=False, skip_group_check=True)
                    if j == 0:
                        pe.wait_ge(sem(f"e_lo{a}"), c + 1 + EU * i)
                    pe.matmul(acc[:, 0:SCALERS * P], lo, w_hi, start=False, stop=False, skip_group_check=True)
                if j == 0:
                    pe.wait_ge(sem("e_std"), c + 1 + EU * i)
                pe.matmul(acc[:, 0:SCALERS * P], agg_sd[:, c % 2, cols], comb_sd[:].rearrange("p s f -> p (s f)"),
                          start=False, stop=False, skip_group_check=True)
                for h, w in ((hdt, comb_x_lo), (hdl, comb_x_hi), (hdt, comb_x_hi)):
                    mm = pe.matmul(acc[:, 0:P], h[:, c % 2, cols], w[:], start=False, stop=(w is comb_x_hi and h is hdt),
                                   skip_group_check=True)
                mm.then_inc(sem("e_layer0"), 1)

            def edge_step(k, i):
                c = k + 1
                if edge(c):
                    pe.wait_ge(sem("e_norm1"), c + 1 + EU * i)
                    if c == 0:
                        pe.wait_ge(sem("n_ht"), NODE_CHUNKS)
                        pe.wait_ge(sem("n_x1"), NODE_CHUNKS)
                    if c >= 3:
                        pe.wait_ge(sem("e_h2l"), c - 2 + EU * i)
                    for j in range(TILES):
                        mm = pe.transpose(bank[0][:, j * P:(j + 1) * P], hs[:, c % 2, j, :], ident[:])
                    mm.then_inc(sem("e_turned_s"), 1)
                    pe.wait_ge(sem("e_norm1d"), c + 1 + EU * i)
                    if c >= 3:
                        pe.wait_ge(sem("e_ut"), 2 * (c - 2) + 2 * EU * i)
                    for j in range(TILES):
                        mm = pe.transpose(bank[1][:, j * P:(j + 1) * P], hd[:, c % 2, j, :], ident[:])
                    mm.then_inc(sem("e_turned_d"), 1)
                c = k
                if edge(c):
                    pe.wait_ge(sem(f"e_attr_in{c % 2}"),
                               16 * (c // 2 + 1) + 8 * EU * i + (16 if c == EDGE_CHUNKS - 1 else 0))
                    if c == 0:
                        pe.wait_ge(sem("n_h2l"), NODE_CHUNKS)
                    if c >= 1:
                        pe.wait_ge(sem("e_attr_run"), c + EU * i)
                    for j in range(TILES):
                        mm = pe.transpose(bank[2][:, j * P:(j + 1) * P], attr[:, c % 2, j, :], ident[:])
                    mm.then_inc(sem("e_turned_attr"), 1)
                    layer0(c, 0, i)
                c = k + 1
                if edge(c):
                    pe.wait_ge(sem("e_hst"), c + 1 + EU * i)
                    if c >= 1:
                        pe.wait_ge(sem("e_sum"), c + EU * i)
                        pe.wait_ge(sem("e_bsq"), c + EU * i)
                    pe.matmul(bank[3][:], ws_t[:], hst[:, c % 2, :], start=True, stop=True).then_inc(sem("e_b_psum"), 1)
                    pe.wait_ge(sem("e_hdt"), c + 1 + EU * i)
                    if c >= 1:
                        pe.wait_ge(sem(f"e_whole{ME}"), c + EU * i)
                    pe.matmul(bank[4][:], wd_lo[:], hdt[:, c % 2, :], start=True, stop=False)
                    pe.matmul(bank[4][:], wd_hi[:], hdt[:, c % 2, :], start=False, stop=False)
                    pe.wait_ge(sem("e_hdl"), c + 1 + EU * i)
                    pe.matmul(bank[4][:], wd_hi[:], hdl[:, c % 2, :], start=False, stop=True).then_inc(sem("e_a_psum"), 1)
                c = k
                if edge(c):
                    layer0(c, 1, i)
                c = k - 1
                if edge(c):
                    pe.wait_ge(sem("e_norm2"), c + 1 + EU * i)
                    if not edge(k + 1) and c >= 1:
                        pe.wait_ge(sem("e_h2l"), c + EU * i)
                    for j in range(TILES):
                        mm = pe.transpose(bank[0][:, j * P:(j + 1) * P], h2[:, c % 2, j, :], ident[:])
                    mm.then_inc(sem("e_turned2"), 1)
                c = k
                if edge(c):
                    layer0(c, 2, i)
                c = k - 1
                if edge(c):
                    pe.wait_ge(sem("e_h2t"), c + 1 + EU * i)
                    pe.wait_ge(sem("e_attr_mean"), c + 1 + EU * i)
                    if c >= 1:
                        pe.wait_ge(sem("e_out"), c + EU * i)
                    for m, b in ((0, 7), (1, 1)):
                        if c >= 1:
                            pe.wait_ge(sem("e_ut"), 2 * c - 1 + m + 2 * EU * i)
                        cols = slice(m * P, (m + 1) * P)
                        pe.matmul(bank[b][:], w1_attr[:, cols], attr_mean[:, c % 2, :], start=True, stop=False)
                        pe.matmul(bank[b][:], w1_lo[:, 0, cols], h2t[:, c % 2, :], start=False, stop=False)
                        pe.matmul(bank[b][:], w1_hi[:, 0, cols], h2t[:, c % 2, :], start=False, stop=False)
                        if m == 0:
                            pe.wait_ge(sem("e_h2l"), c + 1 + EU * i)
                        pe.matmul(bank[b][:], w1_hi[:, 0, cols], h2l[:, c % 2, :], start=False,
                                  stop=True).then_inc(sem("e_u_psum"), 1)
                c = k
                if edge(c):
                    layer0(c, 3, i)
                c = k - 1
                if edge(c):
                    pe.wait_ge(sem("e_ut"), 2 * (c + 1) + 2 * EU * i)
                    pe.matmul(bank[7][:], ones[:], b2_rows[:], start=True, stop=False, skip_group_check=True)
                    for j in range(TILES):
                        for m in range(2):
                            mm = pe.matmul(bank[7][:, j * P:(j + 1) * P], ut[:, c % 2, m, j * P:(j + 1) * P], w2_sb[:, m, :],
                                           start=False, stop=(m == 1), skip_group_check=True)
                    mm.then_inc(sem("e_out_psum"), 1)

            run_passes(pe, node_step, edge_step)

        @block.scalar
        def _(act):
            act.wait_ge(sem("count_ready"), 1)
            act.activation(to_turn[0:ROWS, 3, :], count[0:ROWS, :], ACT.Ln, bias=1.0).then_inc(sem("amp_ready"), 1)
            act.wait_ge(sem("eps_ready"), 1)

            def node_step(k, i):
                c = k
                if node(c):
                    act.wait_ge(sem("n_mv2"), c + 1 + NU * i)
                    if c >= 2:
                        act.wait_ge(sem("n_rs2"), c - 1 + NU * i)
                    act.activation(nsd2[:, c % 2, :], nmv2[:, c % 2, :, 1], ACT.Sqrt, bias=eps_col[:]).then_inc(sem("n_sd2"), 1)
                c = k + 1
                if node(c):
                    act.wait_ge(sem("n_turn1"), c + 1 + NU * i)
                    if c >= 2:
                        act.wait_ge(sem("n_y_psum"), c - 1 + NU * i)
                    act.activation(nht[:, c % 2, :], bank[0][:], ACT.Relu).then_inc(sem("n_ht"), 1)
                c = k - 1
                if node(c):
                    act.wait_ge(sem("n_turn2"), c + 1 + NU * i)
                    if c >= 2:
                        act.wait_ge(sem("n_u_psum"), 2 * (c - 1) + 2 * NU * i)
                    act.activation(nh2t[:, c % 2, :], bank[2][:], ACT.Relu).then_inc(sem("n_h2t"), 1)
                c = k + 3
                if node(c):
                    act.wait_ge(sem("n_mv1"), c + 1 + NU * i)
                    if c >= 2:
                        act.wait_ge(sem("n_rs1"), c - 1 + NU * i)
                    act.activation(nsd1[:, c % 2, :], nmv1[:, c % 4, :, 1], ACT.Sqrt, bias=eps_col[:]).then_inc(sem("n_sd1"), 1)
                c = k
                if node(c):
                    b = c % 2
                    act.wait_ge(sem("n_ms2"), c + 1 + NU * i)
                    if c >= 2:
                        act.wait_ge(sem("n_turn2"), c - 1 + NU * i)
                    for j in range(TILES):
                        last = act.activation(nh2[:, b, j, :], nx1[:, b, j, :], ACT.Identity,
                                              scale=nrs2[:, b, j:j + 1], bias=nms2[:, b, j:j + 1])
                    last.then_inc(sem("n_norm2"), 1)
                c = k + 2
                if node(c):
                    act.wait_ge(sem("n_ms1"), c + 1 + NU * i)
                    if c >= 2:
                        act.wait_ge(sem("n_turn1"), c - 1 + NU * i)
                    act.activation(nh[:, c % 2, 1, :], nx[:, c % 4, 1, :], ACT.Identity,
                                   scale=nrs1[:, c % 4, 1:2], bias=nms1[:, c % 4, :]).then_inc(sem("n_norm1_act"), 1)
                c = k - 2
                if node(c):
                    for m in range(2):
                        act.wait_ge(sem("n_u_psum"), 2 * c + m + 1 + 2 * NU * i)
                        if c >= 2:
                            act.wait_ge(sem("n_out_psum"), c - 1 + NU * i)
                        act.activation(nut[:, c % 2, m, :], bank[6 + m][:], ACT.Relu, bias=b1_col[:, m:m + 1]).then_inc(sem("n_ut"), 1)

            def edge_step(k, i):
                c = k - 1
                if edge(c):
                    act.wait_ge(sem("e_mv2"), c + 1 + EU * i)
                    if c >= 2:
                        act.wait_ge(sem("e_rs2"), c - 1 + EU * i)
                    act.activation(sd2[:, c % 2, :], mv2[:, c % 2, :, 1], ACT.Sqrt, bias=eps_col[:]).then_inc(sem("e_sd2"), 1)
                c = k + 1
                if edge(c):
                    act.wait_ge(sem("e_turned_s"), c + 1 + EU * i)
                    if c == 0:
                        act.wait_ge(sem("n_y_psum"), NODE_CHUNKS)
                    if c >= 2:
                        act.wait_ge(sem("e_b_psum"), c - 1 + EU * i)
                    act.activation(hst[:, c % 2, :], bank[0][:], ACT.Relu).then_inc(sem("e_hst"), 1)
                    act.wait_ge(sem("e_turned_d"), c + 1 + EU * i)
                    if c >= 2:
                        act.wait_ge(sem("e_layer0"), TILES * (c - 1) + TILES * EU * i)
                    act.activation(hdt[:, c % 2, :], bank[1][:], ACT.Relu).then_inc(sem("e_hdt"), 1)
                c = k - 1
                if edge(c):
                    b = c % 2
                    act.wait_ge(sem("e_ms2"), c + 1 + EU * i)
                    if c >= 2:
                        act.wait_ge(sem("e_turned2"), c - 1 + EU * i)
                    for j in range(TILES):
                        last = act.activation(h2[:, b, j, :], x1[:, b, j, :], ACT.Identity,
                                              scale=rs2[:, b, j:j + 1], bias=ms2[:, b, j:j + 1])
                    last.then_inc(sem("e_norm2"), 1)
                c = k + 2
                if edge(c):
                    act.wait_ge(sem("e_mv1"), c + 1 + EU * i)
                    if c >= 2:
                        act.wait_ge(sem("e_rs1"), c - 1 + EU * i)
                    act.activation(sd1[:, c % 2, :], mv1[:, c % 2, :, 1], ACT.Sqrt, bias=eps_col[:]).then_inc(sem("e_sd1"), 1)
                c = k + 1
                if edge(c):
                    act.wait_ge(sem("e_b_psum"), c + 1 + EU * i)
                    if c >= 2:
                        act.wait_ge(sem("e_sqsum"), c - 1 + EU * i)
                    act.activation(bsq[:, c % 2, :], bank[3][:], ACT.Square).then_inc(sem("e_bsq"), 1)
                def norm1(h, rows, first_tile, done):
                    c = k + 2
                    for j in range(TILES):
                        t = first_tile + j
                        last = act.activation(h[:, c % 2, j, :], rows[:, c % 4, j, :], ACT.Identity,
                                              scale=rs1[:, c % 2, t:t + 1], bias=ms1[:, c % 2, t:t + 1])
                    last.then_inc(done, 1)

                c = k + 2
                if edge(c):
                    act.wait_ge(sem("e_ms1"), c + 1 + EU * i)
                    if c == 0:
                        act.wait_ge(sem("n_turn1"), NODE_CHUNKS)
                    if c >= 2:
                        act.wait_ge(sem("e_turned_d"), c - 1 + EU * i)
                    norm1(hs, xs, 0, sem("e_norm1"))
                c = k - 1
                if edge(c):
                    act.wait_ge(sem("e_turned2"), c + 1 + EU * i)
                    if c >= 2:
                        act.wait_ge(sem("e_u_psum"), 2 * (c - 1) + 2 * EU * i)
                    act.activation(h2t[:, c % 2, :], bank[0][:], ACT.Relu).then_inc(sem("e_h2t"), 1)
                if edge(k + 2):
                    norm1(hd, xd, TILES, sem("e_norm1d"))

                def high_part(a, rows):
                    c = k + 1
                    act.wait_ge(sem(f"e_whole{a}"), c + 1 + EU * i)
                    if c >= 2:
                        act.wait_ge(sem("e_layer0"), TILES * (c - 1) + TILES * EU * i)
                    act.activation(agg_hi[:, c % 2, a, :], rows, ACT.Copy).then_inc(sem(f"e_hi{a}"), 1)

                def hidden(m, b):
                    c = k - 1
                    act.wait_ge(sem("e_u_psum"), 2 * c + m + 1 + 2 * EU * i)
                    if c >= 2:
                        act.wait_ge(sem("e_out_psum"), c - 1 + EU * i)
                    act.activation(ut[:, c % 2, m, :], bank[b][:], ACT.Relu, bias=b1_col[:, m:m + 1]).then_inc(sem("e_ut"), 1)

                if edge(k - 1):
                    hidden(0, 7)
                c = k + 1
                if edge(c):
                    act.wait_ge(sem("e_mean_b"), c + 1 + EU * i)
                    if c >= 1:
                        act.wait_ge(sem("e_var"), c + EU * i)
                    act.activation(mean_b2[:], mean_b[:], ACT.Square).then_inc(sem("e_mean_b2"), 1)
                    high_part(MX, whole[:, MX, :])
                if edge(k - 1):
                    hidden(1, 1)
                c = k + 1
                if edge(c):
                    high_part(MN, whole[:, MN, :])
                    act.wait_ge(sem("e_var"), c + 1 + EU * i)
                    act.activation(var[:], var[:], ACT.Relu).then_inc(sem("e_var_pos"), 1)
                    high_part(ME, mean_b[:])
                    act.wait_ge(sem("e_var_pos"), c + 1 + EU * i)
                    act.activation(agg_sd[:, c % 2, :], var[:], ACT.Sqrt, bias=eps_col[:]).then_inc(sem("e_std"), 1)

            run_passes(act, node_step, edge_step)

        @block.vector
        def _(dve):
            chain = sem("dve_setup")
            done = [0]

            def after(ins):
                ins.then_inc(chain, 1)
                done[0] += 1
                dve.wait_ge(chain, done[0])

            dve.memset(dst_i, FAR)
            dve.memset(src_i, 0).then_inc(sem("pad_written"), 1)
            dve.memset(eps_col[:], LN_EPS).then_inc(sem("eps_ready"), 1)
            log2 = math.log(2.0)
            for s, v in enumerate((1.0, log2, 1.0 / log2)):
                last = dve.memset(lone_std[:, s, :], math.sqrt(STD_EPS) * v)
            last.then_inc(sem("lone_std_ready"), 1)
            dve.wait_ge(sem("weights_turned"), 1)
            dve.tensor_copy(w_lin_t[:], bank[0][:, 0:P])
            dve.tensor_copy(wd_t[:], bank[0][:, P:2 * P])
            dve.tensor_copy(ws_t[:], bank[0][:, 2 * P:3 * P]).then_inc(sem("weights_copied"), 1)
            dve.wait_ge(sem("weights_in"), 16 * 13)
            dve.tensor_copy(w1_attr[:], w1_sb[:, 1, :])
            dve.wait_ge(sem("weights_copied"), 1)
            dve.tensor_copy(wd_hi[:], wd_t[:])
            after(dve.tensor_copy(w1_hi[:], w1_sb))
            dve.tensor_tensor(wd_lo[:], wd_t[:], wd_hi[:], ALU.subtract)
            dve.tensor_tensor(w1_lo[:], w1_sb, w1_hi[:], ALU.subtract).then_inc(sem("w1_split"), 1)
            dve.tensor_copy(b_post_wide[:], b_post_col[:].to_broadcast([P, P])).then_inc(sem("b_post_ready"), 1)
            dve.wait_ge(sem("comb_ready"), 1)
            dve.tensor_copy(comb_x[:], bank[1][:, 0:P])
            blocks = [((b - 1) // AGGS, (b - 1) % AGGS, bank[1 + b // 4][:, b % 4 * P:(b % 4 + 1) * P]) for b in range(1, 13)]
            for s, a, block_psum in blocks:
                to = comb_sd[:, s, :] if a == SD else comb_hi[:, a, s, :]
                last = dve.tensor_copy(to, block_psum)
            last.then_inc(sem("comb_copied"), 1)
            dve.wait_ge(sem("comb_copied"), 1)
            after(dve.tensor_copy(comb_x_hi[:], comb_x[:]))
            dve.tensor_tensor(comb_x_lo[:], comb_x[:], comb_x_hi[:], ALU.subtract)
            for s, a, block_psum in blocks:
                if a != SD:
                    last = dve.tensor_tensor(comb_lo[:, a, s, :], block_psum, comb_hi[:, a, s, :], ALU.subtract)
            last.then_inc(sem("comb_split"), 1)
            dve.wait_ge(sem("const_psum"), 1)
            for j in range(TILES):
                last = dve.tensor_tensor(edge_const[:, j, :], bank[5][:, 0:P], b_lin_all[:], ALU.add)
                last.then_inc(sem("const_ready"), 1)
            dve.wait_ge(sem("const_ready"), TILES)
            dve.wait_ge(sem("const_psum"), 2)
            for j in range(TILES):
                last = dve.tensor_tensor(lone_const[:, j, :], bank[6][:, 0:P], edge_const[:, j, :], ALU.add)
                last.then_inc(sem("const_ready"), 1)

            dve.wait_ge(sem("lone_std_ready"), 1)
            dve.tensor_scalar(ones[:], lone_std[0:PAIR, 0, :], 0.0, 1.0, ALU.mult, ALU.add)
            b2_wide = b2_all[:].rearrange("p j f -> p (j f)")
            dve.tensor_copy(b2_hi[:], b2_wide[0:PAIR])
            after(dve.tensor_scalar(b2_rows[:], b2_wide[0:PAIR], 0.0, None, ALU.mult))
            dve.tensor_copy(b2_rows[0:1, :], b2_hi[0:1, :])
            dve.tensor_tensor(b2_rows[LOW:LOW + 1, :], b2_wide[LOW:LOW + 1], b2_hi[LOW:LOW + 1, :],
                              ALU.subtract).then_inc(sem("b2_rows_ready"), 1)

            R = slice(0, ROWS)
            dve.wait_ge(sem("edge_list_in"), 16 * 5)
            dve.wait_ge(sem("pos_ready"), 1)
            dve.tensor_copy(pos1[R], pos_i[R])
            dve.tensor_copy(to_turn[R, 0, :], src_i[R]).then_inc(sem("to_turn_ready"), 1)
            after(dve.tensor_copy(dst_f[R], dst_i[R]))
            dve.tensor_scalar(to_turn[R, 1, :], dst_f[R, 1:RW + 1], float(N - 1), None, ALU.min).then_inc(sem("to_turn_ready"), 1)
            dve.tensor_tensor(first[R], dst_f[R, 1:RW + 1], dst_f[R, 0:RW], ALU.not_equal)
            after(dve.tensor_tensor(final[R], dst_f[R, 1:RW + 1], dst_f[R, 2:RW + 2], ALU.not_equal))
            dve.tensor_scalar(keep_sb[R], first[R], -1.0, 1.0, ALU.mult, ALU.add)
            dve.tensor_scalar(reset_sb[R], first[R], RESET, None, ALU.mult)
            dve.tensor_scalar(lift_sb[R], first[R], -RESET, None, ALU.mult)
            after(dve.tensor_tensor(start_mark[R], first[R], pos1[R], ALU.mult))
            dve.tensor_tensor_scan(start_scan[R], start_mark[R], start_mark[R], 0.0, ALU.max, ALU.max).then_inc(sem("start_scanned"), 1)
            after(dve.tensor_scalar(far_sb[R], pos1[R], float(FAR), None, ALU.add))
            after(dve.tensor_tensor(far_diff[R], dst_f[R, 1:RW + 1], far_sb[R], ALU.subtract))
            after(dve.tensor_tensor(far_pick[R], far_diff[R], final[R], ALU.mult))
            dve.tensor_tensor(to_turn[R, 2, :], far_pick[R], far_sb[R], ALU.add).then_inc(sem("to_turn_ready"), 1)
            dve.memset(row_carry[:], 0.0)
            dve.wait_ge(sem("row_max_psum"), 1)
            after(dve.tensor_copy(row_max[0:1, R], bank[7][0:1, 0:ROWS]))
            dve.tensor_tensor_scan(row_carry[0:1, 1:ROWS], row_max[0:1, 0:ROWS - 1], row_max[0:1, 0:ROWS - 1], 0.0,
                                   ALU.max, ALU.max).then_inc(sem("row_carry_ready"), 1)
            dve.wait_ge(sem("carry_psum"), 1)
            after(dve.tensor_copy(carry_col[R], bank[7][0:ROWS, P:P + 1]))
            after(dve.tensor_scalar(seg_start[R], start_scan[R], carry_col[R], None, ALU.max))
            dve.scalar_tensor_tensor(count[R], pos1[R], 1.0, seg_start[R], ALU.add, ALU.subtract).then_inc(sem("count_ready"), 1)
            dve.wait_ge(sem("count_ready"), 1)
            dve.reciprocal(inv_count[R], count[R]).then_inc(sem("masks_done"), 1)
            dve.wait_ge(sem("amp_ready"), 1)
            dve.reciprocal(to_turn[R, 4, :], to_turn[R, 3, :]).then_inc(sem("to_turn_ready"), 2)
            for n in range(5):
                for h in range(2):
                    dve.wait_ge(sem("turned"), 2 * n + h + 1)
                    to = index[:, n, :, h] if n < 3 else scale[:, n - 3, :, h]
                    dve.tensor_copy(to, bank[h][:, 0:ROWS]).then_inc(sem("turned_out"), 1)

            def node_step(k, i):
                if node(k + 2):
                    c, b = k + 2, k % 2
                    dve.wait_ge(sem("n_sd1"), c + 1 + NU * i)
                    dve.reciprocal(nrs1[:, c % 4, :], nsd1[:, b, :]).then_inc(sem("n_rs1"), 1)
                if node(k + 3):
                    c, b, s = k + 3, (k + 3) % 2, (k + 3) % 4
                    dve.wait_ge(sem(f"n_in{s}"), 16 * (c // 4 + 1) + 16 * i)
                    for j in range(TILES):
                        last = dve.bn_stats(nbn1[:, b, j, :], nx[:, s, j, :])
                    last.then_inc(sem("n_bn1"), 1)
                    dve.wait_ge(sem("n_bn1"), c + 1 + NU * i)
                if node(k):
                    c, b = k, k % 2
                    dve.wait_ge(sem("n_sd2"), c + 1 + NU * i)
                    if c >= 2:
                        dve.wait_ge(sem("n_norm2"), c - 1 + NU * i)
                    dve.reciprocal(nrs2[:, b, :], nsd2[:, b, :]).then_inc(sem("n_rs2"), 1)
                if node(k + 3):
                    c, b = k + 3, (k + 3) % 2
                    if not node(k):
                        dve.memset(stats_go[:], 0.0)
                    for j in range(TILES):
                        last = dve.bn_aggr(nmv1[:, c % 4, j, :], nbn1[:, b, j, :])
                    last.then_inc(sem("n_mv1"), 1)
                if node(k + 2):
                    c = k + 2
                    dve.wait_ge(sem("n_rs1"), c + 1 + NU * i)
                    dve.scalar_tensor_tensor(nms1[:, c % 4, :], nmv1[:, c % 4, 1, 0:1], -1.0, nrs1[:, c % 4, 1:2],
                                             ALU.mult, ALU.mult).then_inc(sem("n_ms1"), 1)
                    if c >= 2:
                        dve.wait_ge(sem("n_turn1"), c - 1 + NU * i)
                    dve.tensor_scalar(nh[:, c % 2, 0, :], nx[:, c % 4, 0, :], nmv1[:, c % 4, 0, 0:1], nrs1[:, c % 4, 0:1],
                                      ALU.subtract, ALU.mult).then_inc(sem("n_norm1"), 1)
                if node(k):
                    b = k % 2
                    dve.wait_ge(sem("n_rs2"), k + 1 + NU * i)
                    dve.scalar_tensor_tensor(nms2[:, b, :], nmv2[:, b, :, 0], -1.0, nrs2[:, b, :],
                                             ALU.mult, ALU.mult).then_inc(sem("n_ms2"), 1)
                if node(k - 1):
                    c = k - 1
                    dve.wait_ge(sem("n_h2t"), c + 1 + NU * i)
                    if c >= 2:
                        dve.wait_ge(sem("n_u_psum"), 2 * (c - 1) + 2 * NU * i)
                    dve.scalar_tensor_tensor(nh2l[:, c % 2, :], bank[2][:], 0.0, nh2t[:, c % 2, :],
                                             ALU.max, ALU.subtract).then_inc(sem("n_h2l"), 1)
                if node(k - 3):
                    c, b = k - 3, (k - 3) % 2
                    dve.wait_ge(sem("n_out_psum"), c + 1 + NU * i)
                    dve.wait_ge(sem("n_x1b"), c + 1 + NU * i)
                    if c >= 2:
                        dve.wait_ge(sem(f"n_stored{b}"), 16 * (c // 2) + 8 * NU * i)
                    dve.tensor_tensor(nout[:, b], bank[5][:].rearrange("p (j f) -> p j f", j=TILES), nx1b[:, c % 4],
                                      ALU.add).then_inc(sem("n_out"), 1)
                if node(k + 1):
                    c, b = k + 1, (k + 1) % 2
                    dve.wait_ge(sem("n_y_psum"), c + 1 + NU * i)
                    dve.wait_ge(sem("n_xc"), c + 1 + NU * i)
                    if c >= 2:
                        dve.wait_ge(sem("n_x1b"), c - 1 + NU * i)
                        dve.wait_ge(sem("n_norm2"), c - 1 + NU * i)
                    dve.tensor_tensor(nx1[:, b], bank[1][:].rearrange("p (j f) -> p j f", j=TILES), nxc[:, b],
                                      ALU.add).then_inc(sem("n_x1"), 1)
                    dve.wait_ge(sem("n_x1"), c + 1 + NU * i)
                    for j in range(TILES):
                        last = dve.bn_stats(nbn2[:, b, j, :], nx1[:, b, j, :])
                    last.then_inc(sem("n_bn2"), 1)
                    dve.wait_ge(sem("n_bn2"), c + 1 + NU * i)
                    dve.memset(stats_go[:], 0.0)
                    for j in range(TILES):
                        last = dve.bn_aggr(nmv2[:, b, j, :], nbn2[:, b, j, :])
                    last.then_inc(sem("n_mv2"), 1)

            def mix_amp(c, j, i):
                acc = bank[5 + j % 2]
                dve.wait_ge(sem("e_layer0"), TILES * c + j + 1 + TILES * EU * i)
                if j == 0:
                    dve.wait_ge(sem("e_xdc"), c + 1 + EU * i)
                    dve.wait_ge(sem("e_scale"), c + 1 + EU * i)
                dve.scalar_tensor_tensor(part[:, j % 2, :], acc[:, P:2 * P], amp_att[:, c % 4, 0, j:j + 1],
                                         xdc[:, c % 2, j, :], ALU.mult, ALU.add).then_inc(sem("e_part"), 1)

            def mix_att(c, j, i):
                acc = bank[5 + j % 2]
                dve.wait_ge(sem("e_part"), TILES * c + j + 1 + TILES * EU * i)
                dve.scalar_tensor_tensor(part2[:, j % 2, :], acc[:, 2 * P:3 * P], amp_att[:, c % 4, 1, j:j + 1],
                                         part[:, j % 2, :], ALU.mult, ALU.add).then_inc(sem("e_part2"), 1)

            def mix_plain(c, j, i):
                acc = bank[5 + j % 2]
                dve.wait_ge(sem("e_part2"), TILES * c + j + 1 + TILES * EU * i)
                if j == 0 and c >= 2:
                    dve.wait_ge(sem("e_norm2"), c - 1 + EU * i)
                dve.tensor_tensor(x1[:, c % 2, j, :], acc[:, 0:P], part2[:, j % 2, :], ALU.add).then_inc(sem("e_mixed"), 1)

            def low_part(a, rows, c, i):
                dve.wait_ge(sem(f"e_hi{a}"), c + 1 + EU * i)
                dve.tensor_tensor(agg_lo[:, c % 2, a, :], rows, agg_hi[:, c % 2, a, :],
                                  ALU.subtract).then_inc(sem(f"e_lo{a}"), 1)

            def edge_step(k, i):
                have, ahead, behind = edge(k), edge(k + 1), edge(k - 1)
                if edge(k - 2):
                    c, b = k - 2, k % 2
                    dve.wait_ge(sem("e_out_psum"), c + 1 + EU * i)
                    if c == 0:
                        for n in range(2):
                            dve.wait_ge(sem(f"n_stored{n}"), 16 * ((NODE_CHUNKS - n + 1) // 2))
                    if c >= 2:
                        dve.wait_ge(sem(f"e_scattered{(c - 2) % 4}"), 16 * TILES * ((c - 2) // 4 + 1) + 16 * TILES * i)
                    dve.tensor_tensor(eout[:, b], bank[7][:].rearrange("p (j f) -> p j f", j=TILES), x1[:, c % 2],
                                      ALU.add).then_inc(sem("e_out"), 1)
                if behind:
                    c, b = k - 1, (k - 1) % 2
                    dve.wait_ge(sem("e_sd2"), c + 1 + EU * i)
                    if c >= 2:
                        dve.wait_ge(sem("e_norm2"), c - 1 + EU * i)
                    dve.reciprocal(rs2[:, b, :], sd2[:, b, :]).then_inc(sem("e_rs2"), 1)
                if edge(k + 2):
                    b, s = k % 2, (k + 2) % 4
                    for j in range(2):
                        dve.bn_stats(bn1[:, b, TILES + j, :], xd[:, s, j, :])
                if behind:
                    c, b = k - 1, (k - 1) % 2
                    dve.wait_ge(sem("e_rs2"), c + 1 + EU * i)
                    dve.scalar_tensor_tensor(ms2[:, b, :], mv2[:, b, :, 0], -1.0, rs2[:, b, :],
                                             ALU.mult, ALU.mult).then_inc(sem("e_ms2"), 1)
                if edge(k + 2):
                    b, s = k % 2, (k + 2) % 4
                    for j in range(2, TILES):
                        last = dve.bn_stats(bn1[:, b, TILES + j, :], xd[:, s, j, :])
                    last.then_inc(sem("e_bn1"), 1)
                    dve.wait_ge(sem("e_bn1"), k + 3 + EU * i)
                if ahead:
                    c, b = k + 1, (k + 1) % 2
                    dve.wait_ge(sem("e_hdt"), c + 1 + EU * i)
                    dve.scalar_tensor_tensor(hdl[:, b, :], bank[1][:], 0.0, hdt[:, b, :],
                                             ALU.max, ALU.subtract).then_inc(sem("e_hdl"), 1)
                elif edge(k + 2):
                    dve.memset(stats_go[:], 0.0)
                if edge(k + 2):
                    b = k % 2
                    for j in range(2 * TILES):
                        last = dve.bn_aggr(mv1[:, b, j, :], bn1[:, b, j, :])
                    last.then_inc(sem("e_mv1"), 1)
                if have:
                    c, b, s = k, k % 2, k % 4
                    dve.wait_ge(sem(f"e_masks_in{s}"), 64 * (c // 4 + 1) + 64 * i)
                    dve.wait_ge(sem("e_turned_attr"), c + 1 + EU * i)
                    if c >= 1:
                        dve.wait_ge(sem("e_attr_run"), c + EU * i)
                    if c >= 2:
                        dve.wait_ge(sem("e_attr_mean"), c - 1 + EU * i)
                    before = run_attr[:, 1 - b, CHUNK - 1:CHUNK] if c else 0.0
                    dve.tensor_tensor_scan(run_attr[:, b, :], keep[:, s, :], bank[2][:], before,
                                           ALU.mult, ALU.add).then_inc(sem("e_attr_run"), 1)
                    mix_amp(c, 0, i)
                if edge(k + 2):
                    c, b = k + 2, k % 2
                    dve.wait_ge(sem("e_sd1"), c + 1 + EU * i)
                    if c >= 2:
                        dve.wait_ge(sem("e_norm1d"), c - 1 + EU * i)
                    dve.reciprocal(rs1[:, b, :], sd1[:, b, :]).then_inc(sem("e_rs1"), 1)
                if have:
                    mix_att(k, 0, i)
                if edge(k + 2):
                    dve.wait_ge(sem("e_rs1"), c + 1 + EU * i)
                    dve.scalar_tensor_tensor(ms1[:, b, :], mv1[:, b, :, 0], -1.0, rs1[:, b, :],
                                             ALU.mult, ALU.mult).then_inc(sem("e_ms1"), 1)
                if have:
                    mix_plain(k, 0, i)
                c, b, s = k + 1, (k + 1) % 2, (k + 1) % 4
                end = slice(CHUNK - 1, CHUNK)
                if ahead:
                    dve.wait_ge(sem("e_bsq"), c + 1 + EU * i)
                    dve.wait_ge(sem(f"e_masks_in{s}"), 64 * (c // 4 + 1) + 64 * i)
                    if c:
                        dve.wait_ge(sem("e_sqsum"), c + EU * i)
                    dve.tensor_tensor_scan(run_max[:, b, :], reset[:, s, :], bank[3][:],
                                           run_max[:, 1 - b, end] if c else 0.0, ALU.add, ALU.max).then_inc(sem("e_max"), 1)
                    dve.tensor_tensor_scan(run_min[:, b, :], lift[:, s, :], bank[3][:],
                                           run_min[:, 1 - b, end] if c else 0.0, ALU.add, ALU.min).then_inc(sem("e_min"), 1)
                    dve.tensor_tensor_scan(run_sum[:, b, :], keep[:, s, :], bank[3][:],
                                           run_sum[:, 1 - b, end] if c else 0.0, ALU.mult, ALU.add).then_inc(sem("e_sum"), 1)
                if behind:
                    p = k - 1
                    dve.wait_ge(sem("e_h2t"), p + 1 + EU * i)
                    if p >= 2:
                        dve.wait_ge(sem("e_u_psum"), 2 * (p - 1) + 2 * EU * i)
                    dve.scalar_tensor_tensor(h2l[:, p % 2, :], bank[0][:], 0.0, h2t[:, p % 2, :],
                                             ALU.max, ALU.subtract).then_inc(sem("e_h2l"), 1)
                if ahead:
                    dve.tensor_tensor_scan(run_sq[:, b, :], keep[:, s, :], bsq[:, b, :],
                                           run_sq[:, 1 - b, end] if c else 0.0, ALU.mult, ALU.add).then_inc(sem("e_sqsum"), 1)
                    dve.wait_ge(sem("e_sum"), c + 1 + EU * i)
                    if c >= 1:
                        dve.wait_ge(sem(f"e_lo{ME}"), c + EU * i)
                    dve.tensor_tensor(mean_b[:], run_sum[:, b, :], inv[:, s, :], ALU.mult).then_inc(sem("e_mean_b"), 1)
                if have:
                    mix_amp(k, 1, i)
                if ahead:
                    dve.wait_ge(sem("e_a_psum"), c + 1 + EU * i)
                    dve.wait_ge(sem("e_max"), c + 1 + EU * i)
                    if c >= 1:
                        dve.wait_ge(sem(f"e_lo{MX}"), c + EU * i)
                    dve.scalar_tensor_tensor(whole[:, MX, :], bank[4][:], b_pre_col[:], run_max[:, b, :],
                                             ALU.add, ALU.add).then_inc(sem(f"e_whole{MX}"), 1)
                if have:
                    mix_att(k, 1, i)
                if ahead:
                    dve.wait_ge(sem("e_min"), c + 1 + EU * i)
                    if c >= 1:
                        dve.wait_ge(sem(f"e_lo{MN}"), c + EU * i)
                    dve.scalar_tensor_tensor(whole[:, MN, :], bank[4][:], b_pre_col[:], run_min[:, b, :],
                                             ALU.add, ALU.add).then_inc(sem(f"e_whole{MN}"), 1)
                if have:
                    mix_plain(k, 1, i)
                if ahead:
                    dve.wait_ge(sem("e_sqsum"), c + 1 + EU * i)
                    if c >= 1:
                        dve.wait_ge(sem("e_std"), c + EU * i)
                    dve.tensor_tensor(var[:], run_sq[:, b, :], inv[:, s, :], ALU.mult).then_inc(sem("e_sq_mean"), 1)
                    dve.wait_ge(sem("e_mean_b2"), c + 1 + EU * i)
                    dve.scalar_tensor_tensor(mean_b[:], bank[4][:], b_pre_col[:], mean_b[:],
                                             ALU.add, ALU.add).then_inc(sem(f"e_whole{ME}"), 1)
                    dve.wait_ge(sem("e_sq_mean"), c + 1 + EU * i)
                    dve.tensor_tensor(var[:], var[:], mean_b2[:], ALU.subtract).then_inc(sem("e_var"), 1)
                if have:
                    mix_amp(k, 2, i)
                if ahead:
                    low_part(ME, mean_b[:], k + 1, i)
                if have:
                    mix_att(k, 2, i)
                    mix_plain(k, 2, i)
                if edge(k + 3):
                    c, b, s = k + 3, (k + 3) % 2, (k + 3) % 4
                    dve.wait_ge(sem(f"e_gathered{s}"), 16 * 2 * TILES * (c // 4 + 1) + 16 * 2 * TILES * i)
                    for j in range(TILES):
                        dve.bn_stats(bn1[:, b, j, :], xs[:, s, j, :])
                if have:
                    c, b = k, k % 2
                    mix_amp(c, 3, i)
                    mix_att(c, 3, i)
                    mix_plain(c, 3, i)
                    dve.wait_ge(sem("e_mixed"), TILES * (c + 1) + TILES * EU * i)
                    for j in range(TILES):
                        last = dve.bn_stats(bn2[:, b, j, :], x1[:, b, j, :])
                    last.then_inc(sem("e_bn2"), 1)
                    dve.wait_ge(sem("e_bn2"), c + 1 + EU * i)
                    dve.memset(stats_go[:], 0.0)
                    for j in range(TILES):
                        last = dve.bn_aggr(mv2[:, b, j, :], bn2[:, b, j, :])
                    last.then_inc(sem("e_mv2"), 1)

            run_passes(dve, node_step, edge_step)


_NAMES = ["x", "src", "dst", "edge_attr_128", "L0_gnn_W_pre", "L0_gnn_b_pre", "L0_gnn_W_post", "L0_gnn_b_post",
          "L0_gnn_W_lin", "L0_gnn_b_lin", "L1_gnn_W1", "L1_gnn_b1", "L1_gnn_W2", "L1_gnn_b2"]


def kernel(**inputs):
    import numpy as np
    import concourse.bacc as bacc
    from concourse.bass_utils import run_bass_kernel_spmd

    nc = bacc.Bacc("TRN2", target_bir_lowering=False, num_devices=1)
    arrays, args = {}, []
    for name in _NAMES:
        a = np.ascontiguousarray(inputs[name])
        arrays[f"in_{name}"] = a
        args.append(nc.dram_tensor(f"in_{name}", a.shape, mybir.dt.from_np(a.dtype), kind="ExternalInput").ap())
    y = nc.dram_tensor("y", arrays["in_x"].shape, mybir.dt.float32, kind="ExternalOutput").ap()
    build(nc, *args, y)
    r = run_bass_kernel_spmd(nc, [arrays], core_ids=[0])
    return r.results[0]["y"]
```
